# Optimizing a Trainium2 kernel written in Bass

```python
import numpy as np
import jax
import jax.numpy as jnp

def _softmax(x, axis=-1):
    return jax.nn.softmax(x, axis=axis)

def _gelu(x):
    return jax.nn.gelu(x, approximate=True)

def _silu(x):
    return jax.nn.silu(x)

def _sigmoid(x):
    return jax.nn.sigmoid(x)

def _layernorm(x, axis=-1, eps=1e-05):
    m = jnp.mean(x, axis=axis, keepdims=True)
    v = jnp.var(x, axis=axis, keepdims=True)
    return (x - m) / jnp.sqrt(v + eps)

def _scatter_add(tgt, idx, src, axis=0):
    return tgt.at[idx].add(src)

def _segment_sum(src, seg, n):
    return jax.ops.segment_sum(src, seg, n)
kernel_name = 'mk_cond_resid_d2_seqx_r4_0cd306'

def setup_inputs(seed: int=0):
    np.random.seed(seed)
    _w = jnp.asarray

    def _rec_inputs():
        import jax
        import jax.numpy as jnp
        _rk = jax.random.key(seed)
        x = -0.000125 + 0.9999 * jax.random.normal(jax.random.fold_in(_rk, 1), (128, 64, 512), jnp.float32)
        _lenS = 64 - jax.random.randint(jax.random.fold_in(_rk, 7), (128,), 0, max(1, 64 // 4) + 1, jnp.int32)
        _lenS2 = 64 - jax.random.randint(jax.random.fold_in(_rk, 8), (128,), 0, max(1, 64 // 4) + 1, jnp.int32)
        itok_B_0_7 = jax.random.randint(jax.random.fold_in(_rk, 11), (128,), 0, 8, jnp.int32)
        fside_8xS_0 = -0.00162727 + 0.0609077 * jax.random.normal(jax.random.fold_in(_rk, 12), (8, 64), jnp.float32)
        itok_B_0_6 = jax.random.randint(jax.random.fold_in(_rk, 13), (128,), 0, 7, jnp.int32)
        return (x, itok_B_0_7, fside_8xS_0, itok_B_0_6)
    x, itok_B_0_7, fside_8xS_0, itok_B_0_6 = _rec_inputs()

    def _L0_cond_setup():
        import jax, jax.numpy as jnp
        import numpy as np
        B, C, T = (64, 64, 512)
        D, N = (64, 8)
        key = jax.random.key(seed)
        k_x, k_s, k_w, k_b = jax.random.split(key, 4)
        scale = 1.0 / np.sqrt(C)
        x = jax.random.normal(k_x, (B, C, T), dtype=jnp.float32)
        subjects = jax.random.randint(k_s, (B,), 0, N, dtype=jnp.int64)
        weights = jax.random.normal(k_w, (N, C, D), dtype=jnp.float32) * scale
        bias = jax.random.normal(k_b, (N, D), dtype=jnp.float32) * scale
        return {'x': x, 'subjects': subjects, 'weights': weights, 'bias': bias}
    _L0_cond_all = _L0_cond_setup()
    _L0_cond_in = {k: v for k, v in _L0_cond_all.items() if k in ('weights',)}
    del _L0_cond_all

    def _L1_cond_setup():
        import jax, jax.numpy as jnp
        import numpy as np
        B, T, D_IN, D_OUT = (16, 512, 512, 512)
        N_ADAPTERS, RANK = (8, 16)
        key = jax.random.key(seed)
        k_x, k_w, k_a, k_b, k_s, k_idx = jax.random.split(key, 6)
        x = jax.random.normal(k_x, (B, T, D_IN), dtype=jnp.float32)
        W = jax.random.normal(k_w, (D_OUT, D_IN), dtype=jnp.float32) * (1.0 / np.sqrt(D_IN))
        A = jax.random.normal(k_a, (N_ADAPTERS, RANK, D_IN), dtype=jnp.float32) * 0.02
        Bm = jax.random.normal(k_b, (N_ADAPTERS, D_OUT, RANK), dtype=jnp.float32) * 0.02
        scalings = jnp.ones((N_ADAPTERS,), dtype=jnp.float32)
        adapter_idx = jax.random.randint(k_idx, (B,), 0, N_ADAPTERS, dtype=jnp.int32)
        return {'x': x, 'W': W, 'A': A, 'Bm': Bm, 'scalings': scalings, 'adapter_idx': adapter_idx}
    _L1_cond_all = _L1_cond_setup()
    _L1_cond_in = {k: v for k, v in _L1_cond_all.items() if k in ('W', 'A', 'Bm', 'scalings')}
    del _L1_cond_all
    return {'x': x, 'itok_B_0_7': itok_B_0_7, 'fside_8xS_0': fside_8xS_0, 'itok_B_0_6': itok_B_0_6, 'L0_cond_weights': _L0_cond_in['weights'], 'L1_cond_W': _L1_cond_in['W'], 'L1_cond_A': _L1_cond_in['A'], 'L1_cond_Bm': _L1_cond_in['Bm'], 'L1_cond_scalings': _L1_cond_in['scalings']}

def reference(x, itok_B_0_7, fside_8xS_0, itok_B_0_6, L0_cond_weights, L1_cond_W, L1_cond_A, L1_cond_Bm, L1_cond_scalings):
    import jax
    import jax.numpy as jnp

    def _L0_cond_ref(x, subjects, weights, bias):
        import jax, jax.numpy as jnp
        import numpy as np
        B, C, T = (64, 64, 512)
        D, N = (64, 8)
        w = weights[subjects]
        b = bias[subjects]
        out = jnp.einsum('bct,bcd->bdt', x, w)
        out = out + b[:, :, None]
        return out

    def _L1_cond_ref(x, W, A, Bm, scalings, adapter_idx):
        import jax, jax.numpy as jnp
        import numpy as np
        B, T, D_IN, D_OUT = (16, 512, 512, 512)
        N_ADAPTERS, RANK = (8, 16)
        H = jnp.einsum('btd,od->bto', x, W)
        A_b = A[adapter_idx]
        B_b = Bm[adapter_idx]
        s_b = scalings[adapter_idx]
        xa = jnp.einsum('btd,brd->btr', x, A_b)
        delta = jnp.einsum('btr,bor->bto', xa, B_b)
        delta = jax.lax.stop_gradient(delta * s_b[:, None, None])
        return H + delta
    x = x + _L0_cond_ref(x, itok_B_0_7, L0_cond_weights, fside_8xS_0)
    x = x + _L1_cond_ref(x, L1_cond_W, L1_cond_A, L1_cond_Bm, L1_cond_scalings, itok_B_0_6)
    return x

_drawn_inputs = setup_inputs


def setup_inputs(seed=0):
    import zlib

    import numpy as np

    out = dict(_drawn_inputs(seed))
    spreads = {'L1_cond_scalings': (1.0, 0.2)}
    factors = {}
    for name, (base, spread) in spreads.items():
        noise = np.random.default_rng([zlib.crc32(name.encode()), seed]).standard_normal(out[name].shape)
        drawn = base * np.exp(spread * noise) if base else spread * noise
        out[name] = jnp.asarray(drawn.astype(out[name].dtype))
    for name, factor in factors.items():
        out[name] = (out[name] * factor).astype(out[name].dtype)
    return out
```

```python
from contextlib import ExitStack

import concourse.bass as bass
from concourse import mybir

F32 = mybir.dt.float32
F32R = mybir.dt.float32r
I32 = mybir.dt.int32
ALU = mybir.AluOpType
ACT = mybir.ActivationFunctionType
AX_X = mybir.AxisListType.X
ds = bass.ds


def cond_residual_layers(nc, x, subject, bias, adapter, w, W, A, Bm, scal, out):
    B, C, T = x.shape
    S = w.shape[0]
    K, R, _ = A.shape
    P = 128
    TC = T // P
    G = 4
    GR = G * R
    assert 2 * C == P and T % P == 0 and T * 4 == 2048 and GR <= 64 and K == S == 8

    PAIRS_MIN = B // 2
    PAIRS = (B + K) // 2
    SLOTS = 2 * PAIRS
    SPARE = SLOTS - B
    XR = 4
    OR = 4

    HEAD = 4
    BODY = 8
    BODIES = (PAIRS_MIN - 16) // BODY
    MID = HEAD + BODY * BODIES
    TAIL = PAIRS - 4
    assert PAIRS_MIN // K == 8 and MID == 52 and TAIL % 4 == 0

    with ExitStack() as ctx:
        def sb(name, shape, dt=F32):
            return ctx.enter_context(nc.sbuf_tensor(name, shape, dt))

        def sem(name):
            return ctx.enter_context(nc.semaphore(name))

        m_hi = sb("m_hi", [P, K * TC * T], F32R)
        m_lo = sb("m_lo", [P, K * TC * T], F32R)
        wt = sb("wt", [P, TC, T])
        b_parts = sb("b_parts", [GR, K * T], F32R)
        b_f = sb("b_f", [GR, 2, T])
        a_f = sb("a_f", [GR, T])
        a_parts = sb("a_parts", [GR, T], F32R)
        b_dup = sb("b_dup", [P, 2, TC, G, R])
        x_ring = sb("x_ring", [P, XR, T])
        o_ring = sb("o_ring", [P, OR, T])
        w_nat = o_ring
        p_all = sb("p_all", [P, S, C])
        bias_all = sb("bias_all", [P, S, C])
        p_pair = sb("p_pair", [P, XR, P])
        bias_pair = sb("bias_pair", [P, XR, P])
        x1 = sb("x1", [P, 2, TC, P])
        x1_hi = sb("x1_hi", [P, 2, TC, P], F32R)
        x1_lo = sb("x1_lo", [P, 2, TC, P], F32R)
        m_f = sb("m_f", [P, T])
        b_nat = m_f[:].rearrange("p (k c r) -> p k c r", k=K, c=TC)
        ident = sb("ident", [P, P])
        before = sb("before", [P, P])
        ones = sb("ones", [P, P])
        scal_all = sb("scal_all", [GR, K])
        neg = sb("neg", [GR, 2])
        iota_i = sb("iota_i", [P, SLOTS], I32)
        iota = sb("iota", [P, SLOTS])
        pid_i = sb("pid_i", [P, 1], I32)
        ids_i = sb("ids_i", [P, 2], I32)
        ids = sb("ids", [P, 2])
        vals = sb("vals", [P, 3])
        onehot = sb("onehot", [P, K])
        cr = sb("cr", [P, 2, K])
        cnt_i = sb("cnt_i", [P, 2, K], I32)
        padded = sb("padded", [P, K])
        key = sb("key", [P, K])
        prec = sb("prec", [P, K, K])
        prec_n = sb("prec_n", [P, K, K])
        start = sb("start", [P, K])
        quant = sb("quant", [P, 4, K])
        quant_b = sb("quant_b", [P, 4])
        small = sb("small", [P, 4])
        place = sb("place", [P, SLOTS])
        place2 = sb("place2", [P, SLOTS])
        spare = sb("spare", [P, SPARE])
        table = sb("table", [1, PAIRS * 8], I32)
        order = sb("order", [1, K], I32)
        order_f = sb("order_f", [1, K])

        ps = ctx.enter_context(nc.psum_tensor("ps", [P, 8, 512], F32))

        ids_in = sem("ids_in")
        w_in = sem("w_in")
        w0_in = sem("w0_in")
        bias_in = sem("bias_in")
        bnat_in = sem("bnat_in")
        scal_in = sem("scal_in")
        consts = sem("consts")
        p_ready = sem("p_ready")
        dve_step = sem("dve_step")
        act_step = sem("act_step")
        oh_ready = sem("oh_ready")
        counted = sem("counted")
        place_ready = sem("place_ready")
        tabled = sem("tabled")
        table_ready = sem("table_ready")
        wt_turned = sem("wt_turned")
        wt_ready = sem("wt_ready")
        b_dupped = sem("b_dupped")
        b_turned = sem("b_turned")
        b_scaled = sem("b_scaled")
        b_rounded = sem("b_rounded")
        b_ready = sem("b_ready")
        a_in = sem("a_in")
        a_rounded = sem("a_rounded")
        a_ready = sem("a_ready")
        m_summed = sem("m_summed")
        m_added = sem("m_added")
        m_hi_ready = sem("m_hi_ready")
        m_ready = sem("m_ready")
        x_in = [sem(f"x_in{i}") for i in range(XR)]
        pair_ready = sem("pair_ready")
        l0_done = sem("l0_done")
        x1_ready = sem("x1_ready")
        x1_hi_ready = sem("x1_hi_ready")
        x1_lo_ready = sem("x1_lo_ready")
        l1_done = sem("l1_done")
        out_ready = sem("out_ready")
        even_out = [sem(f"even_out{i}") for i in range(OR)]
        odd_out = [sem(f"odd_out{i}") for i in range(OR)]

        def at_least(eng, s, v):
            if not isinstance(v, int) or v > 0:
                eng.wait_ge(s, v)

        def pairs(eng, step):
            for j in range(HEAD):
                step(j, j, None)
            with eng.Fori(0, BODIES) as n:
                for u in range(BODY):
                    step(n * BODY + (HEAD + u), (HEAD + u) % 8, n)
            for j in range(MID, MID + 4):
                step(j, j % 8, None)
            with eng.Fori(0, (TAIL - MID - 4) // 4) as q:
                for u in range(4):
                    step(q * 4 + (MID + 4 + u), u, None)
            for j in range(TAIL, PAIRS):
                step(j, j % 8, None)

        def tile_of(j, u, n):
            if u % 2:
                return None
            if n is not None:
                return (n + 1, u // 2) if u >= 4 else (n + 2, u // 2)
            if isinstance(j, int) and j < 7 * 8:
                return 1 + j // 8, u // 2
            return None

        def makes_parts(j, u, n):
            return n + 2 if n is not None and u == 7 else None

        def after(j, u, each):
            return j * (each // XR) + (each - each // XR * (u % XR))

        block = ctx.enter_context(nc.Block())

        @block.sync
        def _(sp):
            with nc.allow_non_contiguous_dma(reason="indices, one per partition"):
                sp.dma_start(ids_i[:, 0:1], adapter.rearrange("(b a) -> b a", a=1)).then_inc(ids_in, 16)
                sp.dma_start(ids_i[:, 1:2], subject.rearrange("(b a) -> b a", a=1)).then_inc(ids_in, 16)
            sp.dma_start(w_nat[:], W.rearrange("(c p) t -> p c t", p=P)).then_inc(w_in, 16)
            sp.dma_start(m_f[:].rearrange("p (k n) -> p k n", k=K), Bm.rearrange("k (p c) r -> p k (c r)", c=TC)).then_inc(bnat_in, 16)
            for half in range(2):
                sp.dma_start(p_all[C * half:C * half + C], w.rearrange("s c d -> c s d")).then_inc(w0_in, 16)
            sp.dma_start(scal_all[:], scal.rearrange("(a k) -> a k", a=1).to_broadcast([GR, K])).then_inc(scal_in, 16)
            sp.dma_start(bias_all[:], bias.rearrange("s d -> (s d)").rearrange("(a n) -> a n", a=1)
                         .to_broadcast([P, S * C]).rearrange("p (s d) -> p s d", s=S)).then_inc(bias_in, 16)

            def load_a(i):
                k = sp.value_load(order[0:1, ds(i, 1)], min_val=0, max_val=K - 1)
                at_least(sp, a_ready, i)
                for g in range(G):
                    sp.dma_start(a_f[R * g:R * g + R, :], A[ds(k, 1)].rearrange("k r t -> (k r) t")
                                 ).then_inc(a_in, 16)

            def batch(j, half):
                return sp.value_load(table[0:1, ds(j * 8 + half, 1)], min_val=0, max_val=B - 1)

            def load_x(j, slot):
                b = [batch(j, half) for half in range(2)]
                at_least(sp, l0_done, j - XR + 1)
                for half in range(2):
                    sp.dma_start(x_ring[C * half:C * half + C, slot, :], x[ds(b[half], 1)].rearrange("b c t -> (b c) t")
                                 ).then_inc(x_in[slot], 16)

            def store(b, slot, half, done):
                sp.dma_start(out[ds(b, 1)].rearrange("b c t -> (b c) t"),
                             o_ring[C * half:C * half + C, slot, :]).then_inc(done[slot], 16)

            sp.wait_ge(table_ready, 1)
            load_a(0)
            for j in range(XR):
                load_x(j, j)
            load_a(1)

            def step(j, u, n):
                if n is not None and u == HEAD:
                    load_a(n + 2)
                even = batch(j, 0)
                odd = batch(j - 1, 1) if not isinstance(j, int) or j > 0 else None
                sp.wait_ge(out_ready, j + 1)
                store(even, u % OR, 0, even_out)
                if not isinstance(j, int) or j > 0:
                    sp.wait_ge(even_out[(u - 1) % OR], after(j - 1, u - 1, 16))
                    store(odd, (u - 1) % OR, 1, odd_out)
                if not isinstance(j, int) or j + XR < PAIRS:
                    load_x(j + XR, u % XR)

            pairs(sp, step)
            odd = batch(PAIRS - 1, 1)
            sp.wait_ge(even_out[(PAIRS - 1) % OR], 16 * (PAIRS // OR))
            store(odd, (PAIRS - 1) % OR, 1, odd_out)
            for slot in range(OR):
                sp.wait_ge(even_out[slot], 16 * (PAIRS // OR))
                sp.wait_ge(odd_out[slot], 16 * (PAIRS // OR))

        @block.gpsimd
        def _(pool):
            nc.gpsimd.iota(iota_i[:], [[1, SLOTS]], base=0, channel_multiplier=0).then_inc(consts, 1)
            nc.gpsimd.iota(pid_i[:], [[0, 1]], base=0, channel_multiplier=1).then_inc(consts, 1)
            nc.gpsimd.memset(ones[:], 1.0).then_inc(consts, 1)
            nc.gpsimd.memset(ident[:], 0.0).then_inc(consts, 1)
            nc.gpsimd.memset(p_pair[:], 0.0).then_inc(consts, 1)
            pool.wait_ge(consts, 5)
            nc.gpsimd.affine_select(out=before[:], in_=ones[:], compare_op=ALU.is_gt, fill=0.0, base=0,
                                    pattern=[[1, P]], channel_multiplier=-1).then_inc(consts, 1)
            nc.gpsimd.affine_select(out=ident[:], in_=ident[:], compare_op=ALU.not_equal, fill=1.0, base=0,
                                    pattern=[[-1, P]], channel_multiplier=1).then_inc(consts, 1)
            nc.gpsimd.memset(neg[:], 0.0).then_inc(consts, 1)
            pool.wait_ge(consts, 8)
            nc.gpsimd.affine_select(out=neg[:, 0:1], in_=neg[:, 0:1], compare_op=ALU.is_gt, fill=-1.0,
                                    base=2 * R, pattern=[[0, 1]], channel_multiplier=-1).then_inc(consts, 1)
            nc.gpsimd.affine_select(out=neg[:, 1:2], in_=neg[:, 1:2], compare_op=ALU.is_gt, fill=-1.0,
                                    base=R, pattern=[[0, 1]], channel_multiplier=-1).then_inc(consts, 1)
            pool.wait_ge(consts, 10)
            nc.gpsimd.affine_select(out=neg[:, 1:2], in_=neg[:, 1:2], compare_op=ALU.is_gt, fill=0.0,
                                    base=2 * R, pattern=[[0, 1]], channel_multiplier=-1).then_inc(consts, 1)
            pool.wait_ge(consts, 11)
            nc.gpsimd.affine_select(out=neg[:, 1:2], in_=neg[:, 1:2], compare_op=ALU.is_gt, fill=-1.0,
                                    base=3 * R, pattern=[[0, 1]], channel_multiplier=-1).then_inc(consts, 1)

            pool.wait_ge(bnat_in, 16)
            for k in range(K):
                at_least(pool, b_turned, k - 1)
                nc.gpsimd.tensor_copy(b_dup[:, k % 2], b_nat[:, k].unsqueeze(2).to_broadcast([P, TC, G, R])
                                      ).then_inc(b_dupped, 1)

            pool.wait_ge(b_dupped, K)
            pool.wait_ge(p_ready, 2)
            pool.wait_ge(bias_in, 16)
            pool.wait_ge(table_ready, 1)

            def step(j, u, n):
                slot = u % XR
                at_least(pool, x1_ready, j - XR + 1)
                s = [pool.value_load(table[0:1, ds(j * 8 + 2 + half, 1)], min_val=0, max_val=S - 1)
                     for half in range(2)]
                def place_p(half):
                    rows = slice(C * half, C * half + C)
                    nc.gpsimd.tensor_copy(p_pair[rows, slot, rows], p_all[rows, ds(s[half], 1), :]
                                          .rearrange("p s d -> p (s d)")).then_inc(pair_ready, 1)

                at_least(pool, pair_ready, j * 4)
                place_p(1)
                pool.wait_ge(pair_ready, j * 4 + 1)
                place_p(0)
                for half in range(2):
                    nc.gpsimd.tensor_copy(bias_pair[:, slot, C * half:C * half + C], bias_all[:, ds(s[half], 1), :]
                                          .rearrange("p s d -> p (s d)")).then_inc(pair_ready, 1)

            pairs(pool, step)

        @block.vector
        def _(dve):
            steps = [0]

            def link(ins):
                steps[0] += 1
                ins.then_inc(dve_step, 1)
                dve.wait_ge(dve_step, steps[0])

            dve.wait_ge(consts, 2)
            dve.wait_ge(ids_in, 32)
            nc.vector.tensor_copy(iota[:], iota_i[:]).then_inc(dve_step, 1)
            nc.vector.tensor_copy(vals[:, 0:1], pid_i[:]).then_inc(dve_step, 1)
            steps[0] += 2
            link(nc.vector.tensor_copy(ids[:], ids_i[:]))
            nc.vector.tensor_copy(vals[:, 1:2], ids[:, 1:2]).then_inc(dve_step, 1)
            steps[0] += 1
            nc.vector.tensor_scalar(onehot[:], iota[:, 0:K], ids[:, 0:1], None, ALU.is_equal).then_inc(oh_ready, 1)
            dve.wait_ge(counted, 1)
            link(nc.vector.tensor_copy(cr[:], ps[:, 0, 0:2 * K].rearrange("p (a k) -> p a k", a=2)))
            link(nc.vector.tensor_copy(cnt_i[:, 0], cr[:, 0, :]))
            link(nc.vector.tensor_scalar(cnt_i[:, 1], cnt_i[:, 0], 1, None, ALU.bitwise_and))
            link(nc.vector.tensor_copy(quant[:, 2, :], cnt_i[:, 1]))
            link(nc.vector.tensor_tensor(padded[:], cr[:, 0, :], quant[:, 2, :], ALU.add))
            link(nc.vector.scalar_tensor_tensor(out=key[:], in0=padded[:], scalar=float(K), in1=iota[:, 0:K],
                                                op0=ALU.mult, op1=ALU.subtract))
            link(nc.vector.tensor_tensor(prec[:], key[:].unsqueeze(1).to_broadcast([P, K, K]),
                                         key[:].unsqueeze(2).to_broadcast([P, K, K]), ALU.is_gt))
            link(nc.vector.tensor_tensor(prec_n[:], prec[:], padded[:].unsqueeze(1).to_broadcast([P, K, K]),
                                         ALU.mult))
            link(nc.vector.tensor_reduce(start[:], prec_n[:], AX_X, ALU.add))
            link(nc.vector.tensor_reduce(quant[:, 1, :], prec[:], AX_X, ALU.add))
            link(nc.vector.tensor_tensor(quant[:, 0, :], start[:], cr[:, 1, :], ALU.add))
            link(nc.vector.tensor_tensor(quant[:, 3, :], cr[:, 0, :], cr[:, 1, :], ALU.subtract))
            link(nc.vector.tensor_tensor(prec_n[:], quant[:, 1, :].unsqueeze(1).to_broadcast([P, K, K]),
                                         iota[:, 0:K].unsqueeze(2).to_broadcast([P, K, K]), ALU.is_equal))
            link(nc.vector.tensor_tensor(prec_n[:], prec_n[:], iota[:, 0:K].unsqueeze(1).to_broadcast([P, K, K]),
                                         ALU.mult))
            link(nc.vector.tensor_reduce(order_f[:], prec_n[0:1], AX_X, ALU.add))
            link(nc.vector.tensor_copy(order[:], order_f[:]))
            link(nc.vector.tensor_tensor(quant[:], quant[:], onehot[:].unsqueeze(1).to_broadcast([P, 4, K]),
                                         ALU.mult))
            link(nc.vector.tensor_reduce(quant_b[:], quant[:], AX_X, ALU.add))
            link(nc.vector.tensor_copy(vals[:, 2:3], quant_b[:, 1:2]))
            link(nc.vector.tensor_scalar(small[:, 0:1], quant_b[:, 0:1], 1.0, None, ALU.add))
            link(nc.vector.scalar_tensor_tensor(out=small[:, 1:2], in0=quant_b[:, 3:4], scalar=1.0,
                                                in1=quant_b[:, 2:3], op0=ALU.is_equal, op1=ALU.mult))
            link(nc.vector.tensor_reduce(small[:, 2:3], padded[:], AX_X, ALU.add))
            link(nc.vector.tensor_scalar(place[:], iota[:], quant_b[:, 0:1], None, ALU.is_equal))
            link(nc.vector.tensor_scalar(place2[:], iota[:], small[:, 0:1], small[:, 1:2], ALU.is_equal, ALU.mult))
            link(nc.vector.tensor_tensor(place[:], place[:], place2[:], ALU.add))
            link(nc.vector.tensor_scalar(spare[:], iota[:, B:SLOTS], small[:, 2:3], None, ALU.is_ge))
            link(nc.vector.tensor_tensor(spare[:], spare[:], place[:, 0:SPARE], ALU.mult))
            nc.vector.tensor_tensor(place[:, B:SLOTS], place[:, B:SLOTS], spare[:], ALU.add).then_inc(place_ready, 1)
            dve.wait_ge(tabled, 1)
            tab = table[:].rearrange("a (j e) -> a j e", e=8)
            for m in range(2):
                nc.vector.tensor_copy(tab[:, :, 2 * m:2 * m + 2], ps[0:1, 1, m * SLOTS:(m + 1) * SLOTS]
                                      .rearrange("a (j h) -> a j h", h=2)).then_inc(dve_step, 1)
                steps[0] += 1
            nc.vector.tensor_copy(tab[:, :, 4:5], ps[0:1, 1, 2 * SLOTS:3 * SLOTS]
                                  .rearrange("a (j h) -> a j h", h=2)[:, :, 0:1]).then_inc(dve_step, 1)
            steps[0] += 1
            dve.wait_ge(dve_step, steps[0])
            nc.vector.memset(small[:, 3:4], 0.0).then_inc(table_ready, 1)

            dve.wait_ge(w0_in, 32)
            dve.wait_ge(consts, 7)
            for half in range(2):
                rows = slice(C * half, C * half + C)
                nc.vector.tensor_tensor(p_all[rows], p_all[rows], ident[rows, rows].unsqueeze(1)
                                        .to_broadcast([C, S, C]), ALU.add).then_inc(p_ready, 1)
            for c in range(TC):
                dve.wait_ge(wt_turned, c + 1)
                link(nc.vector.tensor_copy(wt[:, c, :], ps[:, 4 + c, :]))
                nc.vector.tensor_tensor(wt[:, c, c * P:c * P + P], wt[:, c, c * P:c * P + P], ident[:],
                                        ALU.add).then_inc(wt_ready, 1)

            def a_split(i):
                dve.wait_ge(a_rounded, i + 1)
                nc.vector.scalar_tensor_tensor(out=a_parts[:], in0=a_parts[:], scalar=neg[:, 0:1], in1=a_f[:],
                                               op0=ALU.mult, op1=ALU.add).then_inc(a_ready, 1)

            def b_split(k):
                dve.wait_ge(b_rounded, k + 1)
                cols = b_parts[:, k * T:(k + 1) * T]
                nc.vector.scalar_tensor_tensor(out=cols, in0=cols, scalar=neg[:, 1:2], in1=b_f[:, k % 2, :],
                                               op0=ALU.mult, op1=ALU.add).then_inc(b_ready, 1)

            def m_add(t, chunk):
                dve.wait_ge(m_summed, t + 1)
                at_least(dve, m_ready, t)
                nc.vector.tensor_tensor(m_f[:], ps[:, 4 + chunk % 2, :], wt[:, chunk, :], ALU.add).then_inc(m_added, 1)

            def m_split(t):
                dve.wait_ge(m_hi_ready, t + 1)
                cols = ds(t * T, T) if not isinstance(t, int) else slice(t * T, t * T + T)
                nc.vector.tensor_tensor(m_lo[:, cols], m_f[:], m_hi[:, cols], ALU.subtract).then_inc(m_ready, 1)

            def x1_add(j, u):
                dve.wait_ge(l0_done, j + 1)
                at_least(dve, x1_lo_ready, j - 1)
                nc.vector.tensor_tensor(x1[:, u % 2], ps[:, u % 2, :].rearrange("p (c n) -> p c n", c=TC),
                                        bias_pair[:, u % XR, :].unsqueeze(1).to_broadcast([P, TC, P]),
                                        ALU.add).then_inc(x1_ready, 1)

            def x1_split(j, u):
                dve.wait_ge(x1_hi_ready, j + 1)
                nc.vector.tensor_tensor(x1_lo[:, u % 2], x1[:, u % 2], x1_hi[:, u % 2],
                                        ALU.subtract).then_inc(x1_lo_ready, 1)

            dve.wait_ge(consts, 12)
            for k in range(K):
                b_split(k)
                if k == 0:
                    a_split(0)
            dve.wait_ge(wt_ready, TC)
            for c in range(TC):
                m_add(c, c)
                m_split(c)
            a_split(1)
            x1_add(0, 0)
            x1_split(0, 0)

            def step(j, u, n):
                if not isinstance(j, int) or j + 1 < PAIRS:
                    x1_add(j + 1, u + 1)
                    x1_split(j + 1, u + 1)
                if u % 2 and tile_of(j - 1, u - 1, n):
                    order_at, chunk = tile_of(j - 1, u - 1, n)
                    m_split(order_at * TC + chunk)
                if tile_of(j, u, n):
                    order_at, chunk = tile_of(j, u, n)
                    m_add(order_at * TC + chunk, chunk)
                if makes_parts(j, u, n) is not None:
                    a_split(makes_parts(j, u, n))

            pairs(dve, step)

        @block.scalar
        def _(act):
            def a_round(i):
                act.wait_ge(a_in, 16 * G + i * (16 * G))
                at_least(act, m_summed, i * TC)
                nc.scalar.activation(a_parts[:], a_f[:], ACT.Copy).then_inc(a_rounded, 1)

            def m_round(t):
                act.wait_ge(m_added, t + 1)
                cols = ds(t * T, T) if not isinstance(t, int) else slice(t * T, t * T + T)
                nc.scalar.activation(m_hi[:, cols], m_f[:], ACT.Copy).then_inc(m_hi_ready, 1)

            def x1_round(j, u):
                act.wait_ge(x1_ready, j + 1)
                at_least(act, l1_done, j - 1)
                nc.scalar.activation(x1_hi[:, u % 2], x1[:, u % 2], ACT.Copy).then_inc(x1_hi_ready, 1)

            act.wait_ge(scal_in, 16)
            for k in range(K):
                act.wait_ge(b_turned, k + 1)
                at_least(act, b_ready, k - 1)
                nc.scalar.activation(b_f[:, k % 2, :].rearrange("p (n c) -> p n c", c=TC),
                                     ps[0:GR, 2 + k % 2, :].rearrange("p (c n) -> p n c", c=TC), ACT.Copy,
                                     scale=scal_all[:, k:k + 1]).then_inc(b_scaled, 1)
                act.wait_ge(b_scaled, k + 1)
                nc.scalar.activation(b_parts[:, k * T:(k + 1) * T], b_f[:, k % 2, :], ACT.Copy).then_inc(b_rounded, 1)
                if k == 0:
                    a_round(0)
            for c in range(TC):
                m_round(c)
            a_round(1)
            x1_round(0, 0)

            def step(j, u, n):
                if not isinstance(j, int) or j + 1 < PAIRS:
                    x1_round(j + 1, u + 1)
                act.wait_ge(l1_done, j + 1)
                slot = u % OR
                at_least(act, even_out[slot], after(j - OR, u, 16))
                at_least(act, odd_out[slot], after(j - OR, u, 16))
                nc.scalar.activation(o_ring[:, slot, :], ps[:, 2 + u % 2, :], ACT.Copy).then_inc(out_ready, 1)
                if tile_of(j, u, n):
                    order_at, chunk = tile_of(j, u, n)
                    m_round(order_at * TC + chunk)
                if makes_parts(j, u, n) is not None:
                    a_round(makes_parts(j, u, n))

            pairs(act, step)

        @block.tensor
        def _(pe):
            pe.wait_ge(consts, 7)
            pe.wait_ge(oh_ready, 1)
            nc.tensor.matmul(ps[:, 0, 0:K], ones[:], onehot[:], start=True, stop=True)
            nc.tensor.matmul(ps[:, 0, K:2 * K], before[:], onehot[:], start=True, stop=True).then_inc(counted, 1)
            pe.wait_ge(w_in, 16)
            for c in range(TC):
                for o in range(TC):
                    mm = nc.tensor.transpose(ps[:, 4 + c, o * P:o * P + P], w_nat[:, o, c * P:c * P + P], ident[:])
                mm.then_inc(wt_turned, 1)
            pe.wait_ge(place_ready, 1)
            for m in range(3):
                mm = nc.tensor.matmul(ps[0:1, 1, m * SLOTS:(m + 1) * SLOTS], vals[:, m:m + 1], place[:],
                                      start=True, stop=True)
            mm.then_inc(tabled, 1)
            for k in range(K):
                at_least(pe, b_scaled, k - 1)
                pe.wait_ge(b_dupped, k + 1)
                for o in range(TC):
                    mm = nc.tensor.matmul(ps[0:GR, 2 + k % 2, o * P:o * P + P],
                                          b_dup[:, k % 2, o].rearrange("p g r -> p (g r)"), ident[:],
                                          start=True, stop=True)
                mm.then_inc(b_turned, 1)

            def m_product(t, chunk, k):
                at_least(pe, m_added, t - 1)
                nc.tensor.matmul(ps[:, 4 + chunk % 2, :], a_parts[:, chunk * P:chunk * P + P],
                                 b_parts[:, ds(k * T, T)], start=True, stop=True).then_inc(m_summed, 1)

            def layer0(j, u):
                slot = u % XR
                pe.wait_ge(x_in[slot], after(j, u, 32))
                pe.wait_ge(pair_ready, j * 4 + 4)
                at_least(pe, x1_ready, j - 1)
                for c in range(TC):
                    mm = nc.tensor.matmul(ps[:, u % 2, c * P:c * P + P], x_ring[:, slot, c * P:c * P + P],
                                          p_pair[:, slot, :], start=True, stop=True)
                mm.then_inc(l0_done, 1)

            def layer1(j, u, k):
                pe.wait_ge(x1_lo_ready, j + 1)
                at_least(pe, out_ready, j - 1)
                for c in range(TC):
                    for part, m in ((x1_hi, m_hi), (x1_hi, m_lo), (x1_lo, m_hi)):
                        mm = nc.tensor.matmul(ps[:, 2 + u % 2, :], part[:, u % 2, c, :],
                                              m[:, ds(k * (TC * T) + c * T, T)],
                                              start=(c == 0 and part is x1_hi and m is m_hi),
                                              stop=(c == TC - 1 and part is x1_lo))
                mm.then_inc(l1_done, 1)

            pe.wait_ge(table_ready, 1)
            pe.wait_ge(b_ready, K)
            pe.wait_ge(wt_ready, TC)
            pe.wait_ge(a_ready, 1)
            k = pe.value_load(order[0:1, 0:1], min_val=0, max_val=K - 1)
            for c in range(TC):
                m_product(c, c, k)
            layer0(0, 0)
            pe.wait_ge(m_ready, TC)

            def step(j, u, n):
                k = pe.value_load(table[0:1, ds(j * 8 + 4, 1)], min_val=0, max_val=K - 1)
                if tile_of(j, u, n):
                    order_at, chunk = tile_of(j, u, n)
                    adapter_k = pe.value_load(order[0:1, ds(order_at, 1)], min_val=0, max_val=K - 1)
                if not isinstance(j, int) or j + 1 < PAIRS:
                    layer0(j + 1, u + 1)
                if u == 0 and (n is not None or isinstance(j, int) and 0 < j <= PAIRS_MIN - 8):
                    pe.wait_ge(m_ready, (n + 2) * TC if n is not None else TC * (j // 8 + 1))
                layer1(j, u, k)
                if tile_of(j, u, n):
                    pe.wait_ge(a_ready, order_at + 1)
                    m_product(order_at * TC + chunk, chunk, adapter_k)

            pairs(pe, step)


_INS = ['x', 'itok_B_0_7', 'fside_8xS_0', 'itok_B_0_6', 'L0_cond_weights', 'L1_cond_W', 'L1_cond_A', 'L1_cond_Bm',
        'L1_cond_scalings']
_OUTS = [((128, 64, 512), 'float32')]


def kernel(**inputs):
    import numpy as _np
    import concourse.bacc as _bacc
    from concourse import mybir as _mybir
    from concourse.bass_utils import run_bass_kernel_spmd as _run

    nc = _bacc.Bacc("TRN2", target_bir_lowering=False, num_devices=1)
    arrays, args = {}, []
    for name in _INS:
        a = _np.ascontiguousarray(inputs[name])
        arrays[f"in_{name}_dram"] = a
        args.append(nc.dram_tensor(f"in_{name}_dram", a.shape, _mybir.dt.from_np(a.dtype), kind="ExternalInput").ap())
    for i, (shape, dtype) in enumerate(_OUTS):
        dt = _mybir.dt.from_np(_np.dtype(dtype))
        args.append(nc.dram_tensor(f"out_{i}_dram", shape, dt, kind="ExternalOutput").ap())
    cond_residual_layers(nc, *args)
    r = _run(nc, [arrays], core_ids=[0])
    return r.results[0]["out_0_dram"]
```

```python
from contextlib import ExitStack

import concourse.bass as bass
from concourse import mybir

F32 = mybir.dt.float32
F32R = mybir.dt.float32r
BF16 = mybir.dt.bfloat16
I32 = mybir.dt.int32
ALU = mybir.AluOpType
ACT = mybir.ActivationFunctionType
AX_X = mybir.AxisListType.X
ds = bass.ds


def cond_residual_layers(nc, x, subject, bias, adapter, w, W, A, Bm, scal, out):
    B, C, T = x.shape
    S = w.shape[0]
    K, R, _ = A.shape
    P = 128
    TC = T // P
    G = 4
    GR = G * R
    assert 2 * C == P and T % P == 0 and T * 4 == 2048 and GR <= 64 and K == S == 8

    PAIRS_MIN = B // 2
    PAIRS = (B + K) // 2
    SLOTS = 2 * PAIRS
    SPARE = SLOTS - B
    XR = 4
    OR = 4
    AHEAD = 3
    W_BATCH, W_AHEAD, W_SUBJECT, W_PLACE = 0, 2, 4, 6

    HEAD = 4
    BODY = 8
    BODIES = (PAIRS_MIN - 16) // BODY
    MID = HEAD + BODY * BODIES
    TAIL = PAIRS - 4
    assert PAIRS_MIN // K == 8 and MID == 52 and TAIL % 4 == 0

    with ExitStack() as ctx:
        def sb(name, shape, dt=F32):
            return ctx.enter_context(nc.sbuf_tensor(name, shape, dt))

        def sem(name):
            return ctx.enter_context(nc.semaphore(name))

        m_hi = sb("m_hi", [P, K * TC * T], F32R)
        m_lo = sb("m_lo", [P, K * TC * T], F32R)
        wt = sb("wt", [P, TC, T])
        b_parts = sb("b_parts", [P, T], F32R)
        a_f = sb("a_f", [GR, T])
        a_parts = sb("a_parts", [P, T], F32R)
        b_nat = sb("b_nat", [P, K, TC * R])
        b_dup = sb("b_dup", [P, TC, P // R, R])
        x_ring = sb("x_ring", [P, XR, T])
        o_ring = sb("o_ring", [P, OR, T])
        w_nat = o_ring
        p_all = sb("p_all", [P, S, C])
        bias_all = sb("bias_all", [P, S, C])
        p_pair = sb("p_pair", [P, XR, P])
        bias_pair = sb("bias_pair", [P, XR, P])
        x1 = sb("x1", [P, 2, TC, P])
        x1_hi = sb("x1_hi", [P, 2, TC, P], F32R)
        x1_lo = sb("x1_lo", [P, 2, TC, P], F32R)
        m_f = sb("m_f", [P, 2, T])
        ident = sb("ident", [P, P])
        before = sb("before", [P, P])
        ones = sb("ones", [P, P])
        before_b = sb("before_b", [P, P], BF16)
        ones_b = sb("ones_b", [P, P], BF16)
        ident_b = sb("ident_b", [P, P], BF16)
        ident_halves = sb("ident_halves", [P, C])
        scal_all = sb("scal_all", [P, K])
        neg = sb("neg", [P, 2])
        iota_i = sb("iota_i", [P, SLOTS], I32)
        iota = sb("iota", [P, SLOTS])
        pid_i = sb("pid_i", [P, 1], I32)
        ids_i = sb("ids_i", [P, 2], I32)
        ids = sb("ids", [P, 2])
        vals = sb("vals", [P, 3], BF16)
        onehot = sb("onehot", [P, K], BF16)
        cnt_i = sb("cnt_i", [P, 2, K], I32)
        padded = sb("padded", [P, K])
        key = sb("key", [P, K])
        prec = sb("prec", [P, K, K])
        prec_n = sb("prec_n", [P, K, K])
        at_place = sb("at_place", [P, K, K])
        start = sb("start", [P, K])
        quant = sb("quant", [P, 4, K])
        quant_b = sb("quant_b", [P, 4])
        small = sb("small", [P, 4])
        place = sb("place", [P, SLOTS], BF16)
        place2 = sb("place2", [P, SLOTS])
        spare = sb("spare", [P, SPARE])
        table = sb("table", [1, PAIRS * 8], I32)
        order = sb("order", [1, K], I32)
        order_f = sb("order_f", [1, K])

        ps = ctx.enter_context(nc.psum_tensor("ps", [P, 8, 512], F32))
        b_turned_at = ps[:, 6, :].rearrange("p (c n) -> p n c", c=TC)

        ids_in = sem("ids_in")
        subject_in = sem("subject_in")
        w_in = sem("w_in")
        w0_in = sem("w0_in")
        bias_in = sem("bias_in")
        bnat_in = sem("bnat_in")
        scal_in = sem("scal_in")
        consts = sem("consts")
        consts_b = sem("consts_b")
        p_ready = sem("p_ready")
        dve_step = sem("dve_step")
        oh_ready = sem("oh_ready")
        counted = sem("counted")
        place_ready = sem("place_ready")
        batches_tabled = sem("batches_tabled")
        others_tabled = sem("others_tabled")
        order_ready = sem("order_ready")
        batches_ready = sem("batches_ready")
        others_ready = sem("others_ready")
        wt_turned = sem("wt_turned")
        wt_copied = sem("wt_copied")
        b_nat_ready = sem("b_nat_ready")
        b_dupped = sem("b_dupped")
        b_turned = sem("b_turned")
        b_rounded = sem("b_rounded")
        b_ready = sem("b_ready")
        warmed = sem("warmed")
        a_in = sem("a_in")
        a_rounded = sem("a_rounded")
        a_ready = sem("a_ready")
        m_summed = sem("m_summed")
        m_added = sem("m_added")
        m_hi_ready = sem("m_hi_ready")
        m_ready = sem("m_ready")
        x_in = [sem(f"x_in{i}") for i in range(XR)]
        pair_ready = sem("pair_ready")
        l0_done = sem("l0_done")
        x1_ready = sem("x1_ready")
        x1_hi_ready = sem("x1_hi_ready")
        x1_lo_ready = sem("x1_lo_ready")
        l1_done = sem("l1_done")
        out_ready = sem("out_ready")
        even_out = [sem(f"even_out{i}") for i in range(OR)]
        odd_out = [sem(f"odd_out{i}") for i in range(OR)]

        def at_least(eng, s, v):
            if not isinstance(v, int) or v > 0:
                eng.wait_ge(s, v)

        def pairs(eng, step):
            for j in range(HEAD):
                step(j, j, None)
            with eng.Fori(0, BODIES) as n:
                for u in range(BODY):
                    step(n * BODY + (HEAD + u), (HEAD + u) % 8, n)
            for j in range(MID, MID + 4):
                step(j, j % 8, None)
            with eng.Fori(0, (TAIL - MID - 4) // 4) as q:
                for u in range(4):
                    step(q * 4 + (MID + 4 + u), u, None)
            for j in range(TAIL, PAIRS):
                step(j, j % 8, None)

        def tile_of(j, u, n):
            if u % 2:
                return None
            if n is not None:
                return (n + 1, u // 2) if u >= 4 else (n + 2, u // 2)
            if isinstance(j, int) and j < 7 * 8:
                return 1 + j // 8, u // 2
            return None

        def makes_parts(j, u, n):
            if n is None:
                return 1 if isinstance(j, int) and j == 0 else None
            return n + 2 if u == 7 else None

        def turns_b(j, u, n):
            if n is None:
                return 1 if isinstance(j, int) and j == 0 else None
            return n + 2 if u == 5 else None

        def words(eng, regs, where, most):
            eng.load(regs, where)
            return [eng.snap(r, min_val=0, max_val=most) for r in regs]

        def after(j, u, each):
            return j * (each // XR) + (each - each // XR * (u % XR))

        block = ctx.enter_context(nc.Block())

        @block.sync
        def _(sp):
            with nc.allow_non_contiguous_dma(reason="indices, one per partition"):
                sp.dma_start(ids_i[:, 0:1], adapter.rearrange("(b a) -> b a", a=1)).then_inc(ids_in, 16)
            sp.dma_start(w_nat[:], W.rearrange("(c p) t -> p c t", p=P)).then_inc(w_in, 16)
            for half in range(2):
                sp.dma_start(p_all[C * half:C * half + C], w.rearrange("s c d -> c s d")).then_inc(w0_in, 16)
            sp.dma_start(bias_all[:], bias.rearrange("s d -> (s d)").rearrange("(a n) -> a n", a=1)
                         .to_broadcast([P, S * C]).rearrange("p (s d) -> p s d", s=S)).then_inc(bias_in, 16)
            regs = [sp.alloc_register(f"sp_word{i}") for i in range(4)]

            def load_a(i):
                k, = words(sp, regs[:1], order[0:1, ds(i, 1)], K - 1)
                at_least(sp, a_ready, i)
                sp.dma_start(a_f[:], A[ds(k, 1)].to_broadcast([G, R, T])).then_inc(a_in, 16)

            def load_x(j, slot, b):
                at_least(sp, l0_done, j - XR + 1)
                for half in range(2):
                    sp.dma_start(x_ring[C * half:C * half + C, slot, :], x[ds(b[half], 1)]
                                 .rearrange("b c t -> (b c) t")).then_inc(x_in[slot], 16)

            sp.wait_ge(order_ready, 1)
            load_a(0)
            sp.wait_ge(batches_ready, 1)
            for j in range(AHEAD):
                load_x(j, j, words(sp, regs[:2], table[0:1, j * 8:j * 8 + 2], B - 1))
            load_a(1)

            def step(j, u, n):
                more = not isinstance(j, int) or j + AHEAD < PAIRS
                b = words(sp, regs[:4 if more else 1], table[0:1, ds(j * 8, 4 if more else 1)], B - 1)
                if more:
                    load_x(j + AHEAD, (u + AHEAD) % XR, b[W_AHEAD:W_AHEAD + 2])
                sp.wait_ge(out_ready, j + 1)
                sp.dma_start(out[ds(b[0], 1)].rearrange("b c t -> (b c) t"),
                             o_ring[0:C, u % OR, :]).then_inc(even_out[u % OR], 16)
                if n is not None and u == HEAD:
                    load_a(n + 2)

            pairs(sp, step)
            for slot in range(OR):
                sp.wait_ge(even_out[slot], 16 * (PAIRS // OR))
                sp.wait_ge(odd_out[slot], 16 * (PAIRS // OR))

        @block.gpsimd
        def _(pool):
            nc.gpsimd.iota(iota_i[:], [[1, SLOTS]], base=0, channel_multiplier=0).then_inc(consts, 1)
            nc.gpsimd.iota(pid_i[:], [[0, 1]], base=0, channel_multiplier=1).then_inc(consts, 1)
            nc.gpsimd.memset(ones[:], 1.0).then_inc(consts, 1)
            nc.gpsimd.memset(ident[:], 0.0).then_inc(consts, 1)
            nc.gpsimd.memset(p_pair[:], 0.0).then_inc(consts, 1)
            pool.wait_ge(consts, 5)
            nc.gpsimd.affine_select(out=before[:], in_=ones[:], compare_op=ALU.is_gt, fill=0.0, base=0,
                                    pattern=[[1, P]], channel_multiplier=-1).then_inc(consts, 1)
            nc.gpsimd.affine_select(out=ident[:], in_=ident[:], compare_op=ALU.not_equal, fill=1.0, base=0,
                                    pattern=[[-1, P]], channel_multiplier=1).then_inc(consts, 1)
            nc.gpsimd.memset(neg[:], 0.0).then_inc(consts, 1)
            pool.wait_ge(consts, 8)
            nc.gpsimd.affine_select(out=neg[:, 0:1], in_=neg[:, 0:1], compare_op=ALU.is_gt, fill=-1.0,
                                    base=2 * R, pattern=[[0, 1]], channel_multiplier=-1).then_inc(consts, 1)
            nc.gpsimd.affine_select(out=neg[:, 1:2], in_=neg[:, 1:2], compare_op=ALU.is_gt, fill=-1.0,
                                    base=R, pattern=[[0, 1]], channel_multiplier=-1).then_inc(consts, 1)
            pool.wait_ge(consts, 10)
            nc.gpsimd.affine_select(out=neg[:, 1:2], in_=neg[:, 1:2], compare_op=ALU.is_gt, fill=0.0,
                                    base=2 * R, pattern=[[0, 1]], channel_multiplier=-1).then_inc(consts, 1)
            pool.wait_ge(consts, 11)
            nc.gpsimd.affine_select(out=neg[:, 1:2], in_=neg[:, 1:2], compare_op=ALU.is_gt, fill=-1.0,
                                    base=3 * R, pattern=[[0, 1]], channel_multiplier=-1).then_inc(consts, 1)

            nc.gpsimd.memset(b_dup[:], 0.0).then_inc(consts, 1)
            pool.wait_ge(consts, 13)
            nc.gpsimd.memset(a_parts[GR:P, :].bitcast(F32), 0.0).then_inc(consts, 1)
            pool.wait_ge(consts, 14)
            pool.wait_ge(bnat_in, 16)
            pool.wait_ge(scal_in, 16)
            nc.gpsimd.tensor_tensor(b_nat[:], b_nat[:], scal_all[:].unsqueeze(2).to_broadcast([P, K, TC * R]),
                                    ALU.mult).then_inc(b_nat_ready, 1)
            pool.wait_ge(b_nat_ready, 1)
            regs = [pool.alloc_register(f"pool_word{i}") for i in range(2)]

            def dup_b(i):
                k, = words(pool, regs[:1], order[0:1, ds(i, 1)], K - 1)
                at_least(pool, b_turned, i)
                nc.gpsimd.tensor_copy(b_dup[:, :, 0:G, :], b_nat[:, ds(k, 1), :].rearrange("p k (c r) -> p (k c) r", c=TC)
                                      .unsqueeze(2).to_broadcast([P, TC, G, R])).then_inc(b_dupped, 1)

            pool.wait_ge(order_ready, 1)
            dup_b(0)
            pool.wait_ge(w0_in, 32)
            pool.wait_ge(consts_b, 4)
            nc.gpsimd.tensor_tensor(p_all[:], p_all[:], ident_halves[:].unsqueeze(1).to_broadcast([P, S, C]),
                                    ALU.add).then_inc(p_ready, 1)

            pool.wait_ge(b_dupped, 1)
            pool.wait_ge(p_ready, 1)
            pool.wait_ge(bias_in, 16)
            pool.wait_ge(others_ready, 2)

            def step(j, u, n):
                place_at = n + 2 if n is not None and u == HEAD else 1 if isinstance(j, int) and j == 2 else None
                if place_at is not None:
                    dup_b(place_at)
                    pool.wait_ge(b_dupped, place_at + 1)
                slot = u % XR
                at_least(pool, x1_ready, j - XR + 1)
                s = words(pool, regs, table[0:1, ds(j * 8 + W_SUBJECT, 2)], S - 1)
                def place_p(half):
                    rows = slice(C * half, C * half + C)
                    nc.gpsimd.tensor_copy(p_pair[rows, slot, rows], p_all[rows, ds(s[half], 1), :]
                                          .rearrange("p s d -> p (s d)")).then_inc(pair_ready, 1)

                at_least(pool, pair_ready, j * 4)
                place_p(1)
                pool.wait_ge(pair_ready, j * 4 + 1)
                place_p(0)
                for half in range(2):
                    nc.gpsimd.tensor_copy(bias_pair[:, slot, C * half:C * half + C], bias_all[:, ds(s[half], 1), :]
                                          .rearrange("p s d -> p (s d)")).then_inc(pair_ready, 1)
            pairs(pool, step)

        @block.vector
        def _(dve):
            steps = [0]

            def did(ins):
                steps[0] += 1
                ins.then_inc(dve_step, 1)
                return steps[0]

            def need(number):
                dve.wait_ge(dve_step, number)

            def tt(o, a, b, op):
                return did(nc.vector.tensor_tensor(o, a, b, op))

            counts, earlier = ps[:, 0, 0:K], ps[:, 0, K:2 * K]
            over_k = [P, K, K]
            dve.wait_ge(consts, 2)
            iota_done = did(nc.vector.tensor_copy(iota[:], iota_i[:]))
            dve.wait_ge(consts, 7)
            nc.vector.tensor_copy(ones_b[:], ones[:]).then_inc(consts_b, 1)
            nc.vector.tensor_copy(before_b[:], before[:]).then_inc(consts_b, 1)
            nc.vector.tensor_copy(ident_b[:], ident[:]).then_inc(consts_b, 1)
            nc.vector.tensor_tensor(ident_halves[:], ident[:, 0:C], ident[:, C:2 * C], ALU.add).then_inc(consts_b, 1)
            dve.wait_ge(ids_in, 16)
            need(did(nc.vector.tensor_copy(ids[:, 0:1], ids_i[:, 0:1])))
            nc.vector.tensor_scalar(onehot[:], iota[:, 0:K], ids[:, 0:1], None, ALU.is_equal).then_inc(oh_ready, 1)
            did(nc.vector.tensor_copy(vals[:, 0:1], pid_i[:]))
            dve.wait_ge(counted, 1)
            key_done = did(nc.vector.scalar_tensor_tensor(out=key[:], in0=counts, scalar=float(K), in1=iota[:, 0:K],
                                                          op0=ALU.mult, op1=ALU.subtract))
            cnt_done = did(nc.vector.tensor_copy(cnt_i[:, 0], counts))
            need(key_done)
            prec_done = tt(prec[:], key[:].unsqueeze(1).to_broadcast(over_k), key[:].unsqueeze(2).to_broadcast(over_k),
                           ALU.is_gt)
            need(cnt_done)
            odd_done = did(nc.vector.tensor_scalar(cnt_i[:, 1], cnt_i[:, 0], 1, None, ALU.bitwise_and))
            need(prec_done)
            place_of_done = did(nc.vector.tensor_reduce(quant[:, 1, :], prec[:], AX_X, ALU.add))
            need(odd_done)
            padded_done = tt(padded[:], counts, cnt_i[:, 1], ALU.add)
            need(place_of_done)
            at_done = tt(at_place[:], quant[:, 1, :].unsqueeze(1).to_broadcast(over_k),
                         iota[:, 0:K].unsqueeze(2).to_broadcast(over_k), ALU.is_equal)
            need(padded_done)
            prec_n_done = tt(prec_n[:], prec[:], padded[:].unsqueeze(1).to_broadcast(over_k), ALU.mult)
            need(at_done)
            at_done = tt(at_place[:], at_place[:], iota[:, 0:K].unsqueeze(1).to_broadcast(over_k), ALU.mult)
            need(prec_n_done)
            start_done = did(nc.vector.tensor_reduce(start[:], prec_n[:], AX_X, ALU.add))
            need(at_done)
            order_done = did(nc.vector.tensor_reduce(order_f[:], at_place[0:1], AX_X, ALU.add))
            need(start_done)
            tt(quant[:, 0, :], start[:], earlier, ALU.add)
            need(order_done)
            nc.vector.tensor_copy(order[:], order_f[:]).then_inc(order_ready, 1)
            did(nc.vector.tensor_copy(quant[:, 2, :], cnt_i[:, 1]))
            need(did(nc.vector.scalar_tensor_tensor(out=quant[:, 3, :], in0=earlier, scalar=-1.0, in1=cnt_i[:, 0],
                                                    op0=ALU.mult, op1=ALU.add)))
            need(tt(quant[:], quant[:], onehot[:].unsqueeze(1).to_broadcast([P, 4, K]), ALU.mult))
            need(did(nc.vector.tensor_reduce(quant_b[:], quant[:], AX_X, ALU.add)))
            flag_done = did(nc.vector.scalar_tensor_tensor(out=small[:, 0:1], in0=quant_b[:, 3:4], scalar=1.0,
                                                           in1=quant_b[:, 2:3], op0=ALU.is_equal, op1=ALU.mult))
            from_done = did(nc.vector.tensor_scalar(place2[:], iota[:], quant_b[:, 0:1], None, ALU.is_ge))
            need(flag_done)
            last_done = tt(small[:, 1:2], small[:, 0:1], quant_b[:, 0:1], ALU.add)
            total_done = did(nc.vector.tensor_reduce(small[:, 2:3], padded[:], AX_X, ALU.add))
            did(nc.vector.tensor_copy(vals[:, 2:3], quant_b[:, 1:2]))
            dve.wait_ge(subject_in, 16)
            did(nc.vector.tensor_copy(vals[:, 1:2], ids_i[:, 1:2]))
            need(last_done)
            need(did(nc.vector.scalar_tensor_tensor(out=place[:], in0=iota[:], scalar=small[:, 1:2], in1=place2[:],
                                                    op0=ALU.is_le, op1=ALU.mult)))
            need(did(nc.vector.scalar_tensor_tensor(out=spare[:], in0=iota[:, B:SLOTS], scalar=small[:, 2:3],
                                                    in1=place[:, 0:SPARE], op0=ALU.is_ge, op1=ALU.mult)))
            nc.vector.tensor_tensor(place[:, B:SLOTS], place[:, B:SLOTS], spare[:], ALU.add).then_inc(place_ready, 1)
            dve.wait_ge(batches_tabled, 1)
            rows_of = table[:].rearrange("a (j e) -> a j e", e=8)
            batches = ps[0:1, 1, 0:SLOTS].rearrange("a (j h) -> a j h", h=2)
            did(nc.vector.tensor_copy(rows_of[:, :, W_BATCH:W_BATCH + 2], batches))
            need(did(nc.vector.tensor_copy(rows_of[:, 0:PAIRS - AHEAD, W_AHEAD:W_AHEAD + 2], batches[:, AHEAD:, :])))
            nc.vector.memset(small[:, 3:4], 0.0).then_inc(batches_ready, 1)

            def a_split(i):
                dve.wait_ge(a_rounded, i + 1)
                nc.vector.scalar_tensor_tensor(out=a_parts[0:GR, :], in0=a_parts[0:GR, :], scalar=neg[0:GR, 0:1], in1=a_f[:],
                                               op0=ALU.mult, op1=ALU.add).then_inc(a_ready, 1)

            def b_split(i):
                dve.wait_ge(b_rounded, i + 1)
                nc.vector.scalar_tensor_tensor(out=b_parts[:], in0=b_parts[:], scalar=neg[:, 1:2], in1=b_turned_at,
                                               op0=ALU.mult, op1=ALU.add).then_inc(b_ready, 1)

            def m_add(t, chunk):
                dve.wait_ge(m_summed, t + 1)
                at_least(dve, m_ready, t - 1)
                nc.vector.tensor_tensor(m_f[:, chunk % 2], ps[:, 4 + chunk % 2, :], wt[:, chunk, :],
                                        ALU.add).then_inc(m_added, 1)

            def m_split(t, chunk):
                dve.wait_ge(m_hi_ready, t + 1)
                cols = ds(t * T, T) if not isinstance(t, int) else slice(t * T, t * T + T)
                nc.vector.tensor_tensor(m_lo[:, cols], m_f[:, chunk % 2], m_hi[:, cols], ALU.subtract).then_inc(m_ready, 1)

            def x1_add(j, u):
                dve.wait_ge(l0_done, j + 1)
                at_least(dve, x1_lo_ready, j - 1)
                nc.vector.tensor_tensor(x1[:, u % 2], ps[:, u % 2, :].rearrange("p (c n) -> p c n", c=TC),
                                        bias_pair[:, u % XR, :].unsqueeze(1).to_broadcast([P, TC, P]),
                                        ALU.add).then_inc(x1_ready, 1)

            def x1_split(j, u):
                dve.wait_ge(x1_hi_ready, j + 1)
                nc.vector.tensor_tensor(x1_lo[:, u % 2], x1[:, u % 2], x1_hi[:, u % 2],
                                        ALU.subtract).then_inc(x1_lo_ready, 1)

            dve.wait_ge(consts, 14)
            b_split(0)
            a_split(0)
            dve.wait_ge(wt_copied, TC)
            m_add(0, 0)
            m_add(1, 1)
            m_split(0, 0)
            x1_add(0, 0)
            m_add(2, 2)
            m_split(1, 1)
            x1_split(0, 0)
            m_add(3, 3)
            m_split(2, 2)
            m_split(3, 3)

            def step(j, u, n):
                if not isinstance(j, int) or j + 1 < PAIRS:
                    x1_add(j + 1, u + 1)
                    x1_split(j + 1, u + 1)
                if u % 2 and tile_of(j - 1, u - 1, n):
                    place_at, chunk = tile_of(j - 1, u - 1, n)
                    m_split(place_at * TC + chunk, chunk)
                if makes_parts(j, u, n) is not None:
                    a_split(makes_parts(j, u, n))
                    b_split(makes_parts(j, u, n))
                if tile_of(j, u, n):
                    place_at, chunk = tile_of(j, u, n)
                    m_add(place_at * TC + chunk, chunk)

            pairs(dve, step)

        @block.scalar
        def _(act):
            act.dma_start(b_nat[:], Bm.rearrange("k (p c) r -> p k (c r)", c=TC)).then_inc(bnat_in, 16)
            act.dma_start(scal_all[:], scal.rearrange("(a k) -> a k", a=1).to_broadcast([P, K])).then_inc(scal_in, 16)
            with nc.allow_non_contiguous_dma(reason="indices, one per partition"):
                act.dma_start(ids_i[:, 1:2], subject.rearrange("(b a) -> b a", a=1)).then_inc(subject_in, 16)
            reg = act.alloc_register("act_word")
            act.wait_ge(consts, 3)
            nc.scalar.activation(x1[:, 0, 0, 0:1], ones[:, 0:1], ACT.Copy).then_inc(warmed, 1)

            def a_round(i):
                act.wait_ge(a_in, 16 + i * 16)
                at_least(act, m_summed, i * TC)
                nc.scalar.activation(a_parts[0:GR, :], a_f[:], ACT.Copy).then_inc(a_rounded, 1)

            def b_round(i):
                act.wait_ge(b_turned, i + 1)
                at_least(act, m_summed, i * TC)
                nc.scalar.activation(b_parts[:], b_turned_at, ACT.Copy).then_inc(b_rounded, 1)

            def m_round(t, chunk):
                act.wait_ge(m_added, t + 1)
                cols = ds(t * T, T) if not isinstance(t, int) else slice(t * T, t * T + T)
                nc.scalar.activation(m_hi[:, cols], m_f[:, chunk % 2], ACT.Copy).then_inc(m_hi_ready, 1)

            def x1_round(j, u):
                act.wait_ge(x1_ready, j + 1)
                at_least(act, l1_done, j - 1)
                nc.scalar.activation(x1_hi[:, u % 2], x1[:, u % 2], ACT.Copy).then_inc(x1_hi_ready, 1)

            def store_odd(j, u, b):
                act.wait_ge(even_out[u % OR], after(j, u, 16))
                act.dma_start(out[ds(b, 1)].rearrange("b c t -> (b c) t"),
                              o_ring[C:2 * C, u % OR, :]).then_inc(odd_out[u % OR], 16)

            def copy_wt(c):
                act.wait_ge(wt_turned, c + 1)
                nc.scalar.activation(wt[:, c, :], ps[:, 2 + c % 2, :], ACT.Copy).then_inc(wt_copied, 1)

            copy_wt(0)
            b_round(0)
            a_round(0)
            act.wait_ge(others_tabled, 1)
            rows_of = table[:].rearrange("a (j e) -> a j e", e=8)
            nc.scalar.activation(rows_of[:, :, W_SUBJECT:W_SUBJECT + 2], ps[0:1, 7, SLOTS:2 * SLOTS]
                                 .rearrange("a (j h) -> a j h", h=2), ACT.Copy).then_inc(others_ready, 1)
            nc.scalar.activation(rows_of[:, :, W_PLACE:W_PLACE + 1], ps[0:1, 7, 2 * SLOTS:3 * SLOTS]
                                 .rearrange("a (j h) -> a j h", h=2)[:, :, 0:1], ACT.Copy).then_inc(others_ready, 1)
            copy_wt(1)
            copy_wt(2)
            copy_wt(3)
            m_round(0, 0)
            m_round(1, 1)
            act.wait_ge(warmed, 1)
            x1_round(0, 0)
            m_round(2, 2)
            m_round(3, 3)
            act.wait_ge(batches_ready, 1)

            def step(j, u, n):
                first = isinstance(j, int) and j == 0
                if not isinstance(j, int) or j + 1 < PAIRS:
                    x1_round(j + 1, u + 1)
                if makes_parts(j, u, n) is not None:
                    a_round(makes_parts(j, u, n))
                    b_round(makes_parts(j, u, n))
                if not first:
                    b, = words(act, [reg], table[0:1, ds(j * 8 + (W_BATCH + 1 - 8), 1)], B - 1)
                act.wait_ge(l1_done, j + 1)
                at_least(act, even_out[u % OR], after(j - OR, u, 16))
                at_least(act, odd_out[u % OR], after(j - OR, u, 16))
                nc.scalar.activation(o_ring[:, u % OR, :], ps[:, 2 + u % 2, :], ACT.Copy).then_inc(out_ready, 1)
                if tile_of(j, u, n):
                    place_at, chunk = tile_of(j, u, n)
                    m_round(place_at * TC + chunk, chunk)
                if not first:
                    store_odd(j - 1, u - 1, b)

            pairs(act, step)
            b, = words(act, [reg], table[0:1, (PAIRS - 1) * 8 + 1:(PAIRS - 1) * 8 + 2], B - 1)
            store_odd(PAIRS - 1, PAIRS - 1, b)

        @block.tensor
        def _(pe):
            pe.wait_ge(consts_b, 3)
            pe.wait_ge(oh_ready, 1)
            nc.tensor.matmul(ps[:, 0, 0:K], ones_b[:], onehot[:], start=True, stop=True)
            nc.tensor.matmul(ps[:, 0, K:2 * K], before_b[:], onehot[:], start=True, stop=True).then_inc(counted, 1)
            pe.wait_ge(w_in, 16)

            def turn_w(c):
                at_least(pe, wt_copied, c - 1)
                for o in range(TC):
                    nc.tensor.matmul(ps[:, 2 + c % 2, o * P:o * P + P], w_nat[:, o, c * P:c * P + P], ident[:],
                                     is_transpose=True, start=o == 0, stop=False)
                nc.tensor.matmul(ps[:, 2 + c % 2, c * P:c * P + P], ident_b[:], ident_b[:],
                                 start=False, stop=True).then_inc(wt_turned, 1)

            def turn_b(i):
                pe.wait_ge(b_dupped, i + 1)
                at_least(pe, b_ready, i)
                for c in range(TC):
                    mm = nc.tensor.transpose(ps[:, 6, c * P:c * P + P],
                                             b_dup[:, c].rearrange("p g r -> p (g r)"), ident[:])
                mm.then_inc(b_turned, 1)

            turn_w(0)
            turn_b(0)
            pe.wait_ge(place_ready, 1)
            nc.tensor.matmul(ps[0:1, 1, 0:SLOTS], vals[:, 0:1], place[:], start=True, stop=True).then_inc(batches_tabled, 1)
            for m in range(1, 3):
                mm = nc.tensor.matmul(ps[0:1, 7, m * SLOTS:(m + 1) * SLOTS], vals[:, m:m + 1], place[:],
                                      start=True, stop=True)
            mm.then_inc(others_tabled, 1)

            def m_product(t, chunk):
                at_least(pe, m_added, t - 1)
                nc.tensor.matmul(ps[:, 4 + chunk % 2, :], a_parts[:, chunk * P:chunk * P + P], b_parts[:],
                                 start=True, stop=True).then_inc(m_summed, 1)

            def layer0(j, u):
                slot = u % XR
                pe.wait_ge(x_in[slot], after(j, u, 32))
                pe.wait_ge(pair_ready, j * 4 + 4)
                at_least(pe, x1_ready, j - 1)
                for c in range(TC):
                    mm = nc.tensor.matmul(ps[:, u % 2, c * P:c * P + P], x_ring[:, slot, c * P:c * P + P],
                                          p_pair[:, slot, :], start=True, stop=True)
                mm.then_inc(l0_done, 1)

            def layer1(j, u, k, tiles_awaited=False):
                pe.wait_ge(x1_lo_ready, j + 1)
                at_least(pe, out_ready, j - 1)
                for c in range(TC):
                    if tiles_awaited:
                        pe.wait_ge(m_ready, c + 1)
                    for part, m in ((x1_hi, m_hi), (x1_hi, m_lo), (x1_lo, m_hi)):
                        mm = nc.tensor.matmul(ps[:, 2 + u % 2, :], part[:, u % 2, c, :],
                                              m[:, ds(k * (TC * T) + c * T, T)],
                                              start=(c == 0 and part is x1_hi and m is m_hi),
                                              stop=(c == TC - 1 and part is x1_lo))
                mm.then_inc(l1_done, 1)

            turn_w(1)
            turn_w(2)
            pe.wait_ge(a_ready, 1)
            pe.wait_ge(b_ready, 1)
            m_product(0, 0)
            turn_w(3)
            m_product(1, 1)
            layer0(0, 0)
            m_product(2, 2)
            m_product(3, 3)
            pe.wait_ge(others_ready, 2)
            reg = pe.alloc_register("pe_word")

            def step(j, u, n):
                k, = words(pe, [reg], table[0:1, ds(j * 8 + W_PLACE, 1)], K - 1)
                if not isinstance(j, int) or j + 1 < PAIRS:
                    layer0(j + 1, u + 1)
                if turns_b(j, u, n) is not None:
                    turn_b(turns_b(j, u, n))
                if u == 0 and (n is not None or isinstance(j, int) and 0 < j <= PAIRS_MIN - 8):
                    pe.wait_ge(m_ready, (n + 2) * TC if n is not None else TC * (j // 8 + 1))
                layer1(j, u, k, tiles_awaited=isinstance(j, int) and j == 0)
                if tile_of(j, u, n):
                    place_at, chunk = tile_of(j, u, n)
                    pe.wait_ge(a_ready, place_at + 1)
                    pe.wait_ge(b_ready, place_at + 1)
                    m_product(place_at * TC + chunk, chunk)

            pairs(pe, step)


_INS = ['x', 'itok_B_0_7', 'fside_8xS_0', 'itok_B_0_6', 'L0_cond_weights', 'L1_cond_W', 'L1_cond_A', 'L1_cond_Bm',
        'L1_cond_scalings']
_OUTS = [((128, 64, 512), 'float32')]


def kernel(**inputs):
    import numpy as _np
    import concourse.bacc as _bacc
    from concourse import mybir as _mybir
    from concourse.bass_utils import run_bass_kernel_spmd as _run

    nc = _bacc.Bacc("TRN2", target_bir_lowering=False, num_devices=1)
    arrays, args = {}, []
    for name in _INS:
        a = _np.ascontiguousarray(inputs[name])
        arrays[f"in_{name}_dram"] = a
        args.append(nc.dram_tensor(f"in_{name}_dram", a.shape, _mybir.dt.from_np(a.dtype), kind="ExternalInput").ap())
    for i, (shape, dtype) in enumerate(_OUTS):
        dt = _mybir.dt.from_np(_np.dtype(dtype))
        args.append(nc.dram_tensor(f"out_{i}_dram", shape, dt, kind="ExternalOutput").ap())
    cond_residual_layers(nc, *args)
    r = _run(nc, [arrays], core_ids=[0])
    return r.results[0]["out_0_dram"]
```

```python
from contextlib import ExitStack

import concourse.bass as bass
from concourse import mybir

F32 = mybir.dt.float32
F32R = mybir.dt.float32r
BF16 = mybir.dt.bfloat16
I32 = mybir.dt.int32
ALU = mybir.AluOpType
ACT = mybir.ActivationFunctionType
AX_X = mybir.AxisListType.X
ds = bass.ds


def cond_residual_layers(nc, x, subject, bias, adapter, w, W, A, Bm, scal, out):
    B, C, T = x.shape
    S = w.shape[0]
    K, R, _ = A.shape
    P = 128
    TC = T // P
    G = 4
    GR = G * R
    assert 2 * C == P and T % P == 0 and T * 4 == 2048 and GR <= 64 and K == S == 8

    PAIRS = B // 2
    MIXED = K // 2
    XR = 4
    OR = 4
    AHEAD = 4
    W_BATCH, W_AHEAD, W_SUBJECT, W_PLACE = 0, 2, 4, 6

    HEAD = 4
    BODY = 8
    BODIES = K - 2
    TAIL = HEAD + BODY * BODIES
    assert PAIRS == 64 and TAIL % 4 == 0 and TAIL <= PAIRS - MIXED

    with ExitStack() as ctx:
        def sb(name, shape, dt=F32):
            return ctx.enter_context(nc.sbuf_tensor(name, shape, dt))

        def sem(name):
            return ctx.enter_context(nc.semaphore(name))

        m_hi = sb("m_hi", [P, K * TC * T], F32R)
        m_lo = sb("m_lo", [P, K * TC * T], F32R)
        wt = sb("wt", [P, TC, T])
        b_parts = sb("b_parts", [P, T], F32R)
        a_f = sb("a_f", [GR, T])
        a_parts = sb("a_parts", [P, T], F32R)
        b_nat = sb("b_nat", [P, K, TC * R])
        b_dup = sb("b_dup", [P, TC, P // R, R])
        x_ring = sb("x_ring", [P, XR, T])
        o_ring = sb("o_ring", [P, OR, T])
        w_nat = o_ring
        p_all = sb("p_all", [P, S, C])
        bias_all = sb("bias_all", [P, S, C])
        p_pair = sb("p_pair", [P, XR, P])
        bias_pair = sb("bias_pair", [P, XR, P])
        x1 = sb("x1", [P, 2, TC, P])
        x1_hi = sb("x1_hi", [P, 2, TC, P], F32R)
        x1_lo = sb("x1_lo", [P, 2, TC, P], F32R)
        m_f = sb("m_f", [P, 2, T])
        ident = sb("ident", [P, P])
        before = sb("before", [P, P])
        ones = sb("ones", [P, P])
        before_b = sb("before_b", [P, P], BF16)
        ones_b = sb("ones_b", [P, P], BF16)
        ident_b = sb("ident_b", [P, P], BF16)
        ident_halves = sb("ident_halves", [P, C])
        scal_all = sb("scal_all", [P, K])
        neg = sb("neg", [P, 2])
        iota_i = sb("iota_i", [P, B], I32)
        iota = sb("iota", [P, B])
        pid_i = sb("pid_i", [P, 1], I32)
        ids_i = sb("ids_i", [P, 2], I32)
        ids = sb("ids", [P, 2])
        vals = sb("vals", [P, 3], BF16)
        onehot = sb("onehot", [P, K], BF16)
        cnt_i = sb("cnt_i", [P, 2, K], I32)
        even_odd = sb("even_odd", [P, 2, K])
        key = sb("key", [P, K])
        prec = sb("prec", [P, K, K])
        prec_n = sb("prec_n", [P, 2, K, K])
        at_place = sb("at_place", [P, K, K])
        start = sb("start", [P, 2, K])
        last = sb("last", [P, K])
        quant = sb("quant", [P, 3, K])
        quant_b = sb("quant_b", [P, 3])
        small = sb("small", [P, 2])
        place = sb("place", [P, B], BF16)
        table = sb("table", [1, PAIRS * 8], I32)
        order = sb("order", [1, K], I32)
        order_f = sb("order_f", [1, K])

        ps = ctx.enter_context(nc.psum_tensor("ps", [P, 8, 512], F32))
        b_turned_at = ps[:, 6, :].rearrange("p (c n) -> p n c", c=TC)

        ids_in = sem("ids_in")
        subject_in = sem("subject_in")
        w_in = [sem(f"w_in{c}") for c in range(TC)]
        w0_in = sem("w0_in")
        bias_in = sem("bias_in")
        bnat_in = sem("bnat_in")
        scal_in = sem("scal_in")
        consts = sem("consts")
        consts_b = sem("consts_b")
        p_ready = sem("p_ready")
        dve_step = sem("dve_step")
        oh_ready = sem("oh_ready")
        counted = sem("counted")
        place_ready = sem("place_ready")
        batches_tabled = sem("batches_tabled")
        others_tabled = sem("others_tabled")
        order_ready = sem("order_ready")
        batches_ready = sem("batches_ready")
        others_ready = sem("others_ready")
        wt_turned = sem("wt_turned")
        wt_copied = sem("wt_copied")
        b_nat_ready = sem("b_nat_ready")
        b_dupped = sem("b_dupped")
        b_turned = sem("b_turned")
        b_rounded = sem("b_rounded")
        b_ready = sem("b_ready")
        warmed = sem("warmed")
        a_in = sem("a_in")
        a_rounded = sem("a_rounded")
        a_ready = sem("a_ready")
        m_summed = sem("m_summed")
        m_added = sem("m_added")
        m_hi_ready = sem("m_hi_ready")
        m_ready = sem("m_ready")
        x_in = [sem(f"x_in{i}") for i in range(XR)]
        pair_ready = sem("pair_ready")
        l0_done = sem("l0_done")
        x1_ready = sem("x1_ready")
        x1_hi_ready = sem("x1_hi_ready")
        x1_lo_ready = sem("x1_lo_ready")
        l1_done = sem("l1_done")
        out_ready = sem("out_ready")
        out_odd_ready = sem("out_odd_ready")
        even_out = [sem(f"even_out{i}") for i in range(OR)]
        odd_out = [sem(f"odd_out{i}") for i in range(OR)]

        def at_least(eng, s, v):
            if not isinstance(v, int) or v > 0:
                eng.wait_ge(s, v)

        def pairs(eng, step, head=HEAD):
            for j in range(head):
                step(j, j, None)
            with eng.Fori(0, BODIES) as n:
                for u in range(BODY):
                    step(n * BODY + (head + u), (head + u) % 8, n)
            for j in range(head + BODY * BODIES, PAIRS):
                step(j, j % 8, None)

        def tiles_of(j, u, n):
            if n is not None:
                return {5: [(n + 2, 0)], 7: [(n + 2, 1)], 1: [(n + 2, 2)], 3: [(n + 2, 3)]}.get(u, [])
            return {1: [(1, 0)], 2: [(1, 1)], 3: [(1, 2), (1, 3)]}.get(j, [])

        def split_at(j, u, n):
            if n is not None:
                return {4: [(n + 1, 3)], 6: [(n + 2, 0)], 0: [(n + 2, 1)], 2: [(n + 2, 2)]}.get(u, [])
            return {2: [(1, 0)], 3: [(1, 1)], TAIL: [(K - 1, 3)]}.get(j, [])

        def makes_parts(j, u, n):
            if n is None:
                return 1 if j == 0 else None
            return n + 2 if u == HEAD else None

        def n_of_mixed(j):
            return j - (PAIRS - MIXED) if isinstance(j, int) and j >= PAIRS - MIXED else None

        def words(eng, regs, where, most):
            eng.load(regs, where)
            return [eng.snap(r, min_val=0, max_val=most) for r in regs]

        def after(j, u, each):
            return j * (each // XR) + (each - each // XR * (u % XR))

        block = ctx.enter_context(nc.Block())

        @block.sync
        def _(sp):
            with nc.allow_non_contiguous_dma(reason="indices, one per partition"):
                sp.dma_start(ids_i[:, 0:1], adapter.rearrange("(b a) -> b a", a=1)).then_inc(ids_in, 16)
            sp.dma_start(b_nat[:], Bm.rearrange("k (p c) r -> p k (c r)", c=TC)).then_inc(bnat_in, 16)
            for half in range(2):
                sp.dma_start(p_all[C * half:C * half + C], w.rearrange("s c d -> c s d")).then_inc(w0_in, 16)

            def load_w(c):
                cols = slice(c * P, c * P + P)
                sp.dma_start(w_nat[:, :, cols], W[:, cols].rearrange("(o p) t -> p o t", p=P)).then_inc(w_in[c], 16)

            load_w(0)
            load_w(1)
            regs = [sp.alloc_register(f"sp_word{i}") for i in range(4)]

            def load_a(i):
                k, = words(sp, regs[:1], order[0:1, ds(i, 1)], K - 1)
                at_least(sp, a_ready, i)
                sp.dma_start(a_f[:], A[ds(k, 1)].to_broadcast([G, R, T])).then_inc(a_in, 16)

            def load_x(j, slot, b):
                at_least(sp, l0_done, j - XR + 1)
                for half in range(2):
                    sp.dma_start(x_ring[C * half:C * half + C, slot, :], x[ds(b[half], 1)]
                                 .rearrange("b c t -> (b c) t")).then_inc(x_in[slot], 16)

            sp.wait_ge(order_ready, 1)
            load_a(0)
            load_w(2)
            sp.dma_start(bias_all[:], bias.rearrange("s d -> (s d)").rearrange("(a n) -> a n", a=1)
                         .to_broadcast([P, S * C]).rearrange("p (s d) -> p s d", s=S)).then_inc(bias_in, 16)
            load_w(3)
            sp.wait_ge(batches_ready, 1)
            for j in range(AHEAD):
                load_x(j, j, words(sp, regs[:2], table[0:1, j * 8:j * 8 + 2], B - 1))
            load_a(1)

            def step(j, u, n):
                if n is not None and u == HEAD - 1:
                    load_a(n + 2)
                more = not isinstance(j, int) or j + AHEAD < PAIRS
                b = words(sp, regs[:4 if more else 1], table[0:1, ds(j * 8, 4 if more else 1)], B - 1)
                if more:
                    load_x(j + AHEAD, (u + AHEAD) % XR, b[W_AHEAD:W_AHEAD + 2])
                sp.wait_ge(out_ready, j + 1)
                sp.dma_start(out[ds(b[0], 1)].rearrange("b c t -> (b c) t"),
                             o_ring[0:C, u % OR, :]).then_inc(even_out[u % OR], 16)

            pairs(sp, step, HEAD - 1)
            for slot in range(OR):
                sp.wait_ge(even_out[slot], 16 * (PAIRS // OR))
                sp.wait_ge(odd_out[slot], 16 * (PAIRS // OR))

        @block.gpsimd
        def _(pool):
            nc.gpsimd.iota(iota_i[:], [[1, B]], base=0, channel_multiplier=0).then_inc(consts, 1)
            nc.gpsimd.iota(pid_i[:], [[0, 1]], base=0, channel_multiplier=1).then_inc(consts, 1)
            nc.gpsimd.memset(ones[:], 1.0).then_inc(consts, 1)
            nc.gpsimd.memset(ident[:], 0.0).then_inc(consts, 1)
            nc.gpsimd.memset(p_pair[:], 0.0).then_inc(consts, 1)
            pool.wait_ge(consts, 5)
            nc.gpsimd.affine_select(out=before[:], in_=ones[:], compare_op=ALU.is_gt, fill=0.0, base=0,
                                    pattern=[[1, P]], channel_multiplier=-1).then_inc(consts, 1)
            nc.gpsimd.affine_select(out=ident[:], in_=ident[:], compare_op=ALU.not_equal, fill=1.0, base=0,
                                    pattern=[[-1, P]], channel_multiplier=1).then_inc(consts, 1)
            nc.gpsimd.memset(neg[:], 0.0).then_inc(consts, 1)
            pool.wait_ge(consts, 8)
            nc.gpsimd.affine_select(out=neg[:, 0:1], in_=neg[:, 0:1], compare_op=ALU.is_gt, fill=-1.0,
                                    base=2 * R, pattern=[[0, 1]], channel_multiplier=-1).then_inc(consts, 1)
            nc.gpsimd.affine_select(out=neg[:, 1:2], in_=neg[:, 1:2], compare_op=ALU.is_gt, fill=-1.0,
                                    base=R, pattern=[[0, 1]], channel_multiplier=-1).then_inc(consts, 1)
            pool.wait_ge(consts, 10)
            nc.gpsimd.affine_select(out=neg[:, 1:2], in_=neg[:, 1:2], compare_op=ALU.is_gt, fill=0.0,
                                    base=2 * R, pattern=[[0, 1]], channel_multiplier=-1).then_inc(consts, 1)
            pool.wait_ge(consts, 11)
            nc.gpsimd.affine_select(out=neg[:, 1:2], in_=neg[:, 1:2], compare_op=ALU.is_gt, fill=-1.0,
                                    base=3 * R, pattern=[[0, 1]], channel_multiplier=-1).then_inc(consts, 1)

            nc.gpsimd.memset(b_dup[:], 0.0).then_inc(consts, 1)
            pool.wait_ge(consts, 13)
            nc.gpsimd.memset(a_parts[GR:P, :].bitcast(F32), 0.0).then_inc(consts, 1)
            pool.wait_ge(consts, 14)
            pool.wait_ge(bnat_in, 16)
            pool.wait_ge(scal_in, 16)
            nc.gpsimd.tensor_tensor(b_nat[:], b_nat[:], scal_all[:].unsqueeze(2).to_broadcast([P, K, TC * R]),
                                    ALU.mult).then_inc(b_nat_ready, 1)
            pool.wait_ge(b_nat_ready, 1)
            regs = [pool.alloc_register(f"pool_word{i}") for i in range(2)]

            def dup_b(i):
                k, = words(pool, regs[:1], order[0:1, ds(i, 1)], K - 1)
                at_least(pool, b_turned, i)
                nc.gpsimd.tensor_copy(b_dup[:, :, 0:G, :], b_nat[:, ds(k, 1), :].rearrange("p k (c r) -> p (k c) r", c=TC)
                                      .unsqueeze(2).to_broadcast([P, TC, G, R])).then_inc(b_dupped, 1)

            pool.wait_ge(order_ready, 1)
            dup_b(0)
            pool.wait_ge(w0_in, 32)
            pool.wait_ge(consts_b, 4)
            nc.gpsimd.tensor_tensor(p_all[:], p_all[:], ident_halves[:].unsqueeze(1).to_broadcast([P, S, C]),
                                    ALU.add).then_inc(p_ready, 1)

            pool.wait_ge(b_dupped, 1)
            pool.wait_ge(p_ready, 1)
            pool.wait_ge(others_ready, 2)

            def step(j, u, n):
                place_at = n + 2 if n is not None and u == HEAD else 1 if n is None and j == 1 else None
                if place_at is not None:
                    dup_b(place_at)
                    pool.wait_ge(b_dupped, place_at + 1)
                slot = u % XR
                at_least(pool, x1_ready, j - XR + 1)
                s = words(pool, regs, table[0:1, ds(j * 8 + W_SUBJECT, 2)], S - 1)
                def place_p(half):
                    rows = slice(C * half, C * half + C)
                    nc.gpsimd.tensor_copy(p_pair[rows, slot, rows], p_all[rows, ds(s[half], 1), :]
                                          .rearrange("p s d -> p (s d)")).then_inc(pair_ready, 1)

                at_least(pool, pair_ready, j * 4)
                place_p(1)
                pool.wait_ge(pair_ready, j * 4 + 1)
                place_p(0)
                if isinstance(j, int) and j == 0:
                    pool.wait_ge(bias_in, 16)
                for half in range(2):
                    nc.gpsimd.tensor_copy(bias_pair[:, slot, C * half:C * half + C], bias_all[:, ds(s[half], 1), :]
                                          .rearrange("p s d -> p (s d)")).then_inc(pair_ready, 1)
            pairs(pool, step)

        @block.vector
        def _(dve):
            steps = [0]

            def did(ins):
                steps[0] += 1
                ins.then_inc(dve_step, 1)
                return steps[0]

            def need(number):
                dve.wait_ge(dve_step, number)

            def tt(o, a, b, op):
                return did(nc.vector.tensor_tensor(o, a, b, op))

            counts, earlier = ps[:, 0, 0:K], ps[:, 0, K:2 * K]
            over_k = [P, K, K]
            dve.wait_ge(consts, 2)
            iota_done = did(nc.vector.tensor_copy(iota[:], iota_i[:]))
            dve.wait_ge(consts, 7)
            nc.vector.tensor_copy(ones_b[:], ones[:]).then_inc(consts_b, 1)
            nc.vector.tensor_copy(before_b[:], before[:]).then_inc(consts_b, 1)
            nc.vector.tensor_copy(ident_b[:], ident[:]).then_inc(consts_b, 1)
            nc.vector.tensor_tensor(ident_halves[:], ident[:, 0:C], ident[:, C:2 * C], ALU.add).then_inc(consts_b, 1)
            dve.wait_ge(ids_in, 16)
            need(did(nc.vector.tensor_copy(ids[:, 0:1], ids_i[:, 0:1])))
            nc.vector.tensor_scalar(onehot[:], iota[:, 0:K], ids[:, 0:1], None, ALU.is_equal).then_inc(oh_ready, 1)
            dve.wait_ge(counted, 1)
            key_done = did(nc.vector.scalar_tensor_tensor(out=key[:], in0=counts, scalar=float(K), in1=iota[:, 0:K],
                                                          op0=ALU.mult, op1=ALU.subtract))
            cnt_done = did(nc.vector.tensor_copy(cnt_i[:, 0], counts))
            need(key_done)
            prec_done = tt(prec[:], key[:].unsqueeze(1).to_broadcast(over_k), key[:].unsqueeze(2).to_broadcast(over_k),
                           ALU.is_gt)
            need(cnt_done)
            odd_done = did(nc.vector.tensor_scalar(cnt_i[:, 1], cnt_i[:, 0], 1, None, ALU.bitwise_and))
            need(prec_done)
            place_of_done = did(nc.vector.tensor_reduce(quant[:, 1, :], prec[:], AX_X, ALU.add))
            need(odd_done)
            did(nc.vector.tensor_copy(even_odd[:, 1], cnt_i[:, 1]))
            even_done = tt(even_odd[:, 0], counts, cnt_i[:, 1], ALU.subtract)
            need(place_of_done)
            at_done = tt(at_place[:], quant[:, 1, :].unsqueeze(1).to_broadcast(over_k),
                         iota[:, 0:K].unsqueeze(2).to_broadcast(over_k), ALU.is_equal)
            need(even_done)
            prec_n_done = [tt(prec_n[:, h], prec[:], even_odd[:, h].unsqueeze(1).to_broadcast(over_k), ALU.mult)
                           for h in range(2)][-1]
            need(at_done)
            at_done = tt(at_place[:], at_place[:], iota[:, 0:K].unsqueeze(1).to_broadcast(over_k), ALU.mult)
            need(prec_n_done)
            start_done = did(nc.vector.tensor_reduce(start[:].rearrange("p h k -> p (h k)"),
                                                     prec_n[:].rearrange("p h k m -> p (h k) m"), AX_X, ALU.add))
            need(at_done)
            order_done = did(nc.vector.tensor_reduce(order_f[:], at_place[0:1], AX_X, ALU.add))
            need(start_done)
            tt(quant[:, 0, :], start[:, 0], earlier, ALU.add)
            left_done = tt(start[:, 1], start[:, 1], start[:, 0], ALU.subtract)
            need(order_done)
            nc.vector.tensor_copy(order[:], order_f[:]).then_inc(order_ready, 1)
            whole_done = did(nc.vector.tensor_reduce(small[:, 0:1], even_odd[:, 0], AX_X, ALU.add))
            last_done = tt(last[:], even_odd[:, 0], earlier, ALU.is_equal)
            did(nc.vector.tensor_copy(vals[:, 0:1], pid_i[:]))
            need(whole_done)
            need(did(nc.vector.scalar_tensor_tensor(out=start[:, 1], in0=start[:, 1], scalar=small[:, 0:1],
                                                    in1=even_odd[:, 0], op0=ALU.add, op1=ALU.subtract)))
            need(tt(quant[:, 2, :], last[:], start[:, 1], ALU.mult))
            need(tt(quant[:], quant[:], onehot[:].unsqueeze(1).to_broadcast([P, 3, K]), ALU.mult))
            dve.wait_ge(subject_in, 16)
            did(nc.vector.tensor_copy(vals[:, 1:2], ids_i[:, 1:2]))
            need(did(nc.vector.tensor_reduce(quant_b[:], quant[:], AX_X, ALU.add)))
            did(nc.vector.tensor_copy(vals[:, 2:3], quant_b[:, 1:2]))
            nc.vector.tensor_scalar(place[:], iota[:], quant_b[:, 2:3], quant_b[:, 0:1],
                                    ALU.subtract, ALU.is_equal).then_inc(place_ready, 1)
            dve.wait_ge(batches_tabled, 1)
            rows_of = table[:].rearrange("a (j e) -> a j e", e=8)
            batches = ps[0:1, 1, 0:B].rearrange("a (j h) -> a j h", h=2)
            did(nc.vector.tensor_copy(rows_of[:, :, W_BATCH:W_BATCH + 2], batches))
            need(did(nc.vector.tensor_copy(rows_of[:, 0:PAIRS - AHEAD, W_AHEAD:W_AHEAD + 2], batches[:, AHEAD:, :])))
            nc.vector.memset(small[:, 1:2], 0.0).then_inc(batches_ready, 1)

            def a_split(i):
                dve.wait_ge(a_rounded, i + 1)
                nc.vector.scalar_tensor_tensor(out=a_parts[0:GR, :], in0=a_parts[0:GR, :], scalar=neg[0:GR, 0:1], in1=a_f[:],
                                               op0=ALU.mult, op1=ALU.add).then_inc(a_ready, 1)

            def b_split(i):
                dve.wait_ge(b_rounded, i + 1)
                nc.vector.scalar_tensor_tensor(out=b_parts[:], in0=b_parts[:], scalar=neg[:, 1:2], in1=b_turned_at,
                                               op0=ALU.mult, op1=ALU.add).then_inc(b_ready, 1)

            def m_add(t, chunk):
                dve.wait_ge(m_summed, t + 1)
                if isinstance(t, int) and t < TC:
                    dve.wait_ge(wt_copied, t + 1)
                at_least(dve, m_ready, t - 1)
                nc.vector.tensor_tensor(m_f[:, chunk % 2], ps[:, 4 + chunk % 2, :], wt[:, chunk, :],
                                        ALU.add).then_inc(m_added, 1)

            def m_split(t, chunk):
                dve.wait_ge(m_hi_ready, t + 1)
                cols = ds(t * T, T) if not isinstance(t, int) else slice(t * T, t * T + T)
                nc.vector.tensor_tensor(m_lo[:, cols], m_f[:, chunk % 2], m_hi[:, cols], ALU.subtract).then_inc(m_ready, 1)

            def x1_add(j, u):
                dve.wait_ge(l0_done, j + 1)
                at_least(dve, x1_lo_ready, j - 1)
                nc.vector.tensor_tensor(x1[:, u % 2], ps[:, u % 2, :].rearrange("p (c n) -> p c n", c=TC),
                                        bias_pair[:, u % XR, :].unsqueeze(1).to_broadcast([P, TC, P]),
                                        ALU.add).then_inc(x1_ready, 1)

            def x1_split(j, u):
                dve.wait_ge(x1_hi_ready, j + 1)
                nc.vector.tensor_tensor(x1_lo[:, u % 2], x1[:, u % 2], x1_hi[:, u % 2],
                                        ALU.subtract).then_inc(x1_lo_ready, 1)

            dve.wait_ge(consts, 14)
            b_split(0)
            a_split(0)
            m_add(0, 0)
            m_add(1, 1)
            m_split(0, 0)
            x1_add(0, 0)
            m_add(2, 2)
            x1_split(0, 0)
            m_split(1, 1)
            m_add(3, 3)
            m_split(2, 2)
            m_split(3, 3)

            def step(j, u, n):
                if not isinstance(j, int) or j + 1 < PAIRS:
                    x1_add(j + 1, u + 1)
                    x1_split(j + 1, u + 1)
                for place_at, chunk in split_at(j, u, n):
                    m_split(place_at * TC + chunk, chunk)
                if makes_parts(j, u, n) is not None:
                    a_split(makes_parts(j, u, n))
                    b_split(makes_parts(j, u, n))
                for place_at, chunk in tiles_of(j, u, n):
                    m_add(place_at * TC + chunk, chunk)
                if n is None and j == HEAD - 1:
                    m_split(TC + 2, 2)

            pairs(dve, step)

        @block.scalar
        def _(act):
            act.dma_start(scal_all[:], scal.rearrange("(a k) -> a k", a=1).to_broadcast([P, K])).then_inc(scal_in, 16)
            with nc.allow_non_contiguous_dma(reason="indices, one per partition"):
                act.dma_start(ids_i[:, 1:2], subject.rearrange("(b a) -> b a", a=1)).then_inc(subject_in, 16)
            regs = [act.alloc_register(f"act_word{i}") for i in range(3)]
            act.wait_ge(consts, 3)
            nc.scalar.activation(x1[:, 0, 0, 0:1], ones[:, 0:1], ACT.Copy).then_inc(warmed, 1)

            def a_round(i):
                act.wait_ge(a_in, 16 + i * 16)
                at_least(act, m_summed, i * TC)
                nc.scalar.activation(a_parts[0:GR, :], a_f[:], ACT.Copy).then_inc(a_rounded, 1)

            def b_round(i):
                act.wait_ge(b_turned, i + 1)
                at_least(act, m_summed, i * TC)
                nc.scalar.activation(b_parts[:], b_turned_at, ACT.Copy).then_inc(b_rounded, 1)

            def m_round(t, chunk):
                act.wait_ge(m_added, t + 1)
                cols = ds(t * T, T) if not isinstance(t, int) else slice(t * T, t * T + T)
                nc.scalar.activation(m_hi[:, cols], m_f[:, chunk % 2], ACT.Copy).then_inc(m_hi_ready, 1)

            def x1_round(j, u):
                act.wait_ge(x1_ready, j + 1)
                at_least(act, l1_done, j - 1)
                nc.scalar.activation(x1_hi[:, u % 2], x1[:, u % 2], ACT.Copy).then_inc(x1_hi_ready, 1)

            def copy_out(j, u, places):
                at_least(act, even_out[u % OR], after(j - OR, u, 16))
                at_least(act, odd_out[u % OR], after(j - OR, u, 16))
                act.wait_ge(l1_done, j + 1)
                if places is None:
                    nc.scalar.activation(o_ring[:, u % OR, :], ps[:, 2 + u % 2, :], ACT.Copy).then_inc(out_ready, 1)
                    return
                nc.scalar.activation(o_ring[0:C, u % OR, :], ps[0:C, 2 + u % 2, :], ACT.Copy).then_inc(out_ready, 1)
                with act.If_ne(regs[1], regs[2]):
                    nc.scalar.activation(o_ring[C:2 * C, u % OR, :], ps[C:2 * C, 4 + u % 2, :],
                                         ACT.Copy).then_inc(out_odd_ready, 1)
                with act.Else():
                    nc.scalar.activation(o_ring[C:2 * C, u % OR, :], ps[C:2 * C, 2 + u % 2, :],
                                         ACT.Copy).then_inc(out_odd_ready, 1)

            def store_odd(j, u, b):
                if n_of_mixed(j) is None:
                    act.wait_ge(out_ready, j + 1)
                else:
                    act.wait_ge(out_odd_ready, n_of_mixed(j) + 1)
                act.dma_start(out[ds(b, 1)].rearrange("b c t -> (b c) t"),
                              o_ring[C:2 * C, u % OR, :]).then_inc(odd_out[u % OR], 16)

            def copy_wt(c):
                act.wait_ge(wt_turned, c + 1)
                nc.scalar.activation(wt[:, c, :], ps[:, 2 + c % 2, :], ACT.Copy).then_inc(wt_copied, 1)

            act.wait_ge(others_tabled, 1)
            rows_of = table[:].rearrange("a (j e) -> a j e", e=8)
            nc.scalar.activation(rows_of[:, :, W_SUBJECT:W_SUBJECT + 2], ps[0:1, 7, B:2 * B]
                                 .rearrange("a (j h) -> a j h", h=2), ACT.Copy).then_inc(others_ready, 1)
            nc.scalar.activation(rows_of[:, :, W_PLACE:W_PLACE + 2], ps[0:1, 7, 2 * B:3 * B]
                                 .rearrange("a (j h) -> a j h", h=2), ACT.Copy).then_inc(others_ready, 1)
            b_round(0)
            a_round(0)
            copy_wt(0)
            copy_wt(1)
            m_round(0, 0)
            copy_wt(2)
            m_round(1, 1)
            copy_wt(3)
            act.wait_ge(warmed, 1)
            x1_round(0, 0)
            m_round(2, 2)
            m_round(3, 3)
            act.wait_ge(batches_ready, 1)

            def step(j, u, n):
                if not isinstance(j, int) or j + 1 < PAIRS:
                    x1_round(j + 1, u + 1)
                if makes_parts(j, u, n) is not None:
                    a_round(makes_parts(j, u, n))
                    b_round(makes_parts(j, u, n))
                b, = words(act, regs[:1], table[0:1, ds(j * 8 + (W_BATCH + 1), 1)], B - 1)
                places = None
                if n_of_mixed(j) is not None:
                    places = words(act, regs[1:3], table[0:1, ds(j * 8 + W_PLACE, 2)], K - 1)
                copy_out(j, u, places)
                for place_at, chunk in tiles_of(j, u, n):
                    m_round(place_at * TC + chunk, chunk)
                store_odd(j, u, b)

            pairs(act, step)

        @block.tensor
        def _(pe):
            pe.wait_ge(consts_b, 3)
            pe.wait_ge(oh_ready, 1)
            nc.tensor.matmul(ps[:, 0, 0:K], ones_b[:], onehot[:], start=True, stop=True)
            nc.tensor.matmul(ps[:, 0, K:2 * K], before_b[:], onehot[:], start=True, stop=True).then_inc(counted, 1)
            def turn_w(c):
                pe.wait_ge(w_in[c], 16)
                at_least(pe, wt_copied, c - 1)
                for o in range(TC):
                    nc.tensor.matmul(ps[:, 2 + c % 2, o * P:o * P + P], w_nat[:, o, c * P:c * P + P], ident[:],
                                     is_transpose=True, start=o == 0, stop=False)
                nc.tensor.matmul(ps[:, 2 + c % 2, c * P:c * P + P], ident_b[:], ident_b[:],
                                 start=False, stop=True).then_inc(wt_turned, 1)

            def turn_b(i):
                pe.wait_ge(b_dupped, i + 1)
                at_least(pe, b_ready, i)
                for c in range(TC):
                    mm = nc.tensor.transpose(ps[:, 6, c * P:c * P + P],
                                             b_dup[:, c].rearrange("p g r -> p (g r)"), ident[:])
                mm.then_inc(b_turned, 1)

            pe.wait_ge(place_ready, 1)
            nc.tensor.matmul(ps[0:1, 1, 0:B], vals[:, 0:1], place[:], start=True, stop=True).then_inc(batches_tabled, 1)
            for m in range(1, 3):
                mm = nc.tensor.matmul(ps[0:1, 7, m * B:(m + 1) * B], vals[:, m:m + 1], place[:],
                                      start=True, stop=True)
            mm.then_inc(others_tabled, 1)
            turn_b(0)
            turn_w(0)
            turn_w(1)

            def m_product(t, chunk):
                at_least(pe, m_added, t - 1)
                nc.tensor.matmul(ps[:, 4 + chunk % 2, :], a_parts[:, chunk * P:chunk * P + P], b_parts[:],
                                 start=True, stop=True).then_inc(m_summed, 1)

            def layer0(j, u):
                slot = u % XR
                pe.wait_ge(x_in[slot], after(j, u, 32))
                pe.wait_ge(pair_ready, j * 4 + 4)
                at_least(pe, x1_ready, j - 1)
                for c in range(TC):
                    mm = nc.tensor.matmul(ps[:, u % 2, c * P:c * P + P], x_ring[:, slot, c * P:c * P + P],
                                          p_pair[:, slot, :], start=True, stop=True)
                mm.then_inc(l0_done, 1)

            def layer1(j, u, k, bank, done=l1_done, tiles_awaited=False):
                pe.wait_ge(x1_lo_ready, j + 1)
                at_least(pe, out_ready, j - 1)
                if n_of_mixed(j) is not None:
                    at_least(pe, out_odd_ready, n_of_mixed(j) - 1)
                for c in range(TC):
                    if tiles_awaited:
                        pe.wait_ge(m_ready, c + 1)
                    for part, m in ((x1_hi, m_hi), (x1_hi, m_lo), (x1_lo, m_hi)):
                        mm = nc.tensor.matmul(ps[:, bank, :], part[:, u % 2, c, :],
                                              m[:, ds(k * (TC * T) + c * T, T)],
                                              start=(c == 0 and part is x1_hi and m is m_hi),
                                              stop=(c == TC - 1 and part is x1_lo))
                if done is not None:
                    mm.then_inc(done, 1)

            pe.wait_ge(a_ready, 1)
            pe.wait_ge(b_ready, 1)
            m_product(0, 0)
            m_product(1, 1)
            turn_w(2)
            layer0(0, 0)
            turn_w(3)
            m_product(2, 2)
            m_product(3, 3)
            pe.wait_ge(others_ready, 2)
            regs = [pe.alloc_register(f"pe_word{i}") for i in range(2)]

            def step(j, u, n):
                mixed = n_of_mixed(j) is not None
                k = words(pe, regs[:2 if mixed else 1], table[0:1, ds(j * 8 + W_PLACE, 2 if mixed else 1)], K - 1)
                if not isinstance(j, int) or j + 1 < PAIRS:
                    layer0(j + 1, u + 1)
                if makes_parts(j, u, n) is not None:
                    turn_b(makes_parts(j, u, n))
                if n is not None and u == HEAD + 1:
                    pe.wait_ge(m_ready, n * TC + 2 * TC)
                if n is None and j == TAIL + 1:
                    pe.wait_ge(m_ready, K * TC)
                if mixed:
                    with pe.If_ne(regs[0], regs[1]):
                        layer1(j, u, k[1], 4 + u % 2, done=None)
                layer1(j, u, k[0], 2 + u % 2, tiles_awaited=n is None and j == 0)
                for place_at, chunk in tiles_of(j, u, n):
                    pe.wait_ge(a_ready, place_at + 1)
                    pe.wait_ge(b_ready, place_at + 1)
                    m_product(place_at * TC + chunk, chunk)

            pairs(pe, step)


_INS = ['x', 'itok_B_0_7', 'fside_8xS_0', 'itok_B_0_6', 'L0_cond_weights', 'L1_cond_W', 'L1_cond_A', 'L1_cond_Bm',
        'L1_cond_scalings']
_OUTS = [((128, 64, 512), 'float32')]


def kernel(**inputs):
    import numpy as _np
    import concourse.bacc as _bacc
    from concourse import mybir as _mybir
    from concourse.bass_utils import run_bass_kernel_spmd as _run

    nc = _bacc.Bacc("TRN2", target_bir_lowering=False, num_devices=1)
    arrays, args = {}, []
    for name in _INS:
        a = _np.ascontiguousarray(inputs[name])
        arrays[f"in_{name}_dram"] = a
        args.append(nc.dram_tensor(f"in_{name}_dram", a.shape, _mybir.dt.from_np(a.dtype), kind="ExternalInput").ap())
    for i, (shape, dtype) in enumerate(_OUTS):
        dt = _mybir.dt.from_np(_np.dtype(dtype))
        args.append(nc.dram_tensor(f"out_{i}_dram", shape, dt, kind="ExternalOutput").ap())
    cond_residual_layers(nc, *args)
    r = _run(nc, [arrays], core_ids=[0])
    return r.results[0]["out_0_dram"]
```
